# Optimizing a Trainium2 kernel written in Bass

```python
import numpy as np
import jax
import jax.numpy as jnp

def _softmax(x, axis=-1):
    return jax.nn.softmax(x, axis=axis)

def _gelu(x):
    return jax.nn.gelu(x, approximate=True)

def _silu(x):
    return jax.nn.silu(x)

def _sigmoid(x):
    return jax.nn.sigmoid(x)

def _layernorm(x, axis=-1, eps=1e-05):
    m = jnp.mean(x, axis=axis, keepdims=True)
    v = jnp.var(x, axis=axis, keepdims=True)
    return (x - m) / jnp.sqrt(v + eps)

def _scatter_add(tgt, idx, src, axis=0):
    return tgt.at[idx].add(src)

def _segment_sum(src, seg, n):
    return jax.ops.segment_sum(src, seg, n)
kernel_name = 'mk_prb_d1_jaxref_r4_950e2f'

def setup_inputs(seed: int=0):
    np.random.seed(seed)
    _w = jnp.asarray

    def _L0_attn_setup():
        import jax, jax.numpy as jnp
        import numpy as np
        B, S, E, H = (4, 512, 256, 16)
        HD = E // H
        key = jax.random.key(seed)
        ks = jax.random.split(key, 5)
        scale = 1.0 / np.sqrt(E)
        x = jax.random.normal(ks[0], (B, S, E), dtype=jnp.float32)
        Wqkv = jax.random.uniform(ks[1], (E, 3 * E), dtype=jnp.float32, minval=-scale, maxval=scale)
        bqkv = jax.random.uniform(ks[2], (3 * E,), dtype=jnp.float32, minval=-scale, maxval=scale)
        Wout = jax.random.uniform(ks[3], (E, E), dtype=jnp.float32, minval=-scale, maxval=scale)
        bout = jax.random.uniform(ks[4], (E,), dtype=jnp.float32, minval=-scale, maxval=scale)
        return {'x': x, 'Wqkv': Wqkv, 'bqkv': bqkv, 'Wout': Wout, 'bout': bout}
    _L0_attn_in = _L0_attn_setup()

    def _L0_ffn_setup():
        import jax, jax.numpy as jnp
        import numpy as np
        B, S, H, F, E = (4, 512, 256, 1024, 8)
        key = jax.random.key(seed)
        ks = jax.random.split(key, 8)
        s = 1.0 / np.sqrt(H)
        sf = 1.0 / np.sqrt(F)
        return {'x': jax.random.normal(ks[0], (B, S, H), jnp.float32), 'wr': jax.random.uniform(ks[1], (H, E), jnp.float32, -s, s), 'br': jax.random.uniform(ks[2], (E,), jnp.float32, -s, s), 'w1': jax.random.uniform(ks[3], (E, H, F), jnp.float32, -s, s), 'b1': jax.random.uniform(ks[4], (E, F), jnp.float32, -s, s), 'w2': jax.random.uniform(ks[5], (E, F, H), jnp.float32, -sf, sf), 'b2': jax.random.uniform(ks[6], (E, H), jnp.float32, -sf, sf)}
    _L0_ffn_in = _L0_ffn_setup()
    _d = {'L0_attn_x': _L0_attn_in['x'], 'L0_attn_Wqkv': _L0_attn_in['Wqkv'], 'L0_attn_bqkv': _L0_attn_in['bqkv'], 'L0_attn_Wout': _L0_attn_in['Wout'], 'L0_attn_bout': _L0_attn_in['bout'], 'L0_ffn_wr': _L0_ffn_in['wr'], 'L0_ffn_br': _L0_ffn_in['br'], 'L0_ffn_w1': _L0_ffn_in['w1'], 'L0_ffn_b1': _L0_ffn_in['b1'], 'L0_ffn_w2': _L0_ffn_in['w2'], 'L0_ffn_b2': _L0_ffn_in['b2']}
    _x0 = _d['L0_attn_x']
    _d['L0_attn_x'] = jax.random.normal(jax.random.fold_in(jax.random.key(seed), 1), (1, 4096, 256), dtype=_x0.dtype)
    del _x0
    return _d

def reference(L0_attn_x, L0_attn_Wqkv, L0_attn_bqkv, L0_attn_Wout, L0_attn_bout, L0_ffn_wr, L0_ffn_br, L0_ffn_w1, L0_ffn_b1, L0_ffn_w2, L0_ffn_b2):

    def _L0_attn_ref(x, Wqkv, bqkv, Wout, bout):
        import jax, jax.numpy as jnp
        import numpy as np
        B, S, E, H = (4, 512, 256, 16)
        HD = E // H
        b, s, e = x.shape
        qkv = x @ Wqkv + bqkv
        qkv = qkv.reshape(b, s, H, 3 * HD)
        q, k, v = (qkv[..., :HD], qkv[..., HD:2 * HD], qkv[..., 2 * HD:])
        scores = jnp.einsum('bqhd,bkhd->bhqk', q, k) / jnp.sqrt(jnp.float32(HD))
        attn = jax.nn.softmax(scores, axis=-1)
        out = jnp.einsum('bhqk,bkhd->bqhd', attn, v).reshape(b, s, e)
        return out @ Wout + bout

    def _L0_ffn_ref(x, wr, br, w1, b1, w2, b2):
        import jax, jax.numpy as jnp
        import numpy as np
        B, S, H, F, E = (4, 512, 256, 1024, 8)
        scores = jnp.einsum('bsh,he->bse', x, wr) + br
        expert_id = jnp.argmax(scores, axis=-1)
        h = jnp.einsum('bsh,ehf->ebsf', x, w1) + b1[:, None, None, :]
        h = jax.nn.gelu(h, approximate=False)
        y = jnp.einsum('ebsf,efh->ebsh', h, w2) + b2[:, None, None, :]
        one_hot = jax.nn.one_hot(expert_id, E, dtype=x.dtype)
        out = jnp.einsum('ebsh,bse->bsh', y, one_hot)
        return out
    x = L0_attn_x
    xn = _layernorm(x, axis=-1)
    x = x + _L0_attn_ref(xn, L0_attn_Wqkv, L0_attn_bqkv, L0_attn_Wout, L0_attn_bout) + _L0_ffn_ref(xn, L0_ffn_wr, L0_ffn_br, L0_ffn_w1, L0_ffn_b1, L0_ffn_w2, L0_ffn_b2)
    return x

_drawn_inputs = setup_inputs


def setup_inputs(seed=0):
    import zlib

    import numpy as np

    out = dict(_drawn_inputs(seed))
    spreads = {}
    factors = {'L0_attn_Wqkv': 6.394, 'L0_ffn_b1': 4.473, 'L0_ffn_b2': 3.143, 'L0_attn_bout': 3.301}
    for name, (base, spread) in spreads.items():
        noise = np.random.default_rng([zlib.crc32(name.encode()), seed]).standard_normal(out[name].shape)
        drawn = base * np.exp(spread * noise) if base else spread * noise
        out[name] = jnp.asarray(drawn.astype(out[name].dtype))
    for name, factor in factors.items():
        out[name] = (out[name] * factor).astype(out[name].dtype)
    return out
```

```python
import concourse.bass as bass
from concourse import mybir
from contextlib import ExitStack

F32 = mybir.dt.float32
BF16 = mybir.dt.bfloat16
I32 = mybir.dt.int32
ACT = mybir.ActivationFunctionType
ALU = mybir.AluOpType
X_AXIS = mybir.AxisListType.X

P = 128
S = 4096
E = 256
H = 16
D = E // H
KH = E // P
TILES = S // P
EPS = 1e-5
PARTS = 3
SPLIT_ROWS = 6 * D
SHIFT_ROWS = SPLIT_ROWS + PARTS
QB = 512
NQB = S // QB
UNITS = H * NQB
QT = QB // P
KT = S // P
KCHUNK = 1024
NKC = S // KCHUNK
CHUNKS = QT * NKC
ITEMS = CHUNKS + 1
BATCH = 4
NBATCH = KT // BATCH
PV_LAG = 4
LATE = 1 + PV_LAG // BATCH
PBUFS = 16
STBUFS = 3
VCOL = 32
KBUFS = 3
DMA = 16

QUERY_GROUPS = ((0, 3, 0), (3, 2, 1), (5, 1, 2))
KEY_GROUPS = ((0, 3, 0), (3, 2, 0), (5, 1, 0))
N_EXPERTS = 8
F = 1024
FT = F // P
RB = 256
RT = RB // P
BLOCKS = S // RB + N_EXPERTS - 1
SLOTS = BLOCKS * RB
COUNT_STEPS = S // RB


def wait(engine, sem, value):
    if not isinstance(value, int) or value > 0:
        engine.wait_ge(sem, value)


def wait_alone(engine, sem, value, turns):
    wait(engine, sem, value)
    engine.sem_inc(turns, 1)


def ring_base(step):
    return 0 if isinstance(step, int) and step == -2 else 33 + ITEMS * step


def build(nc, x, w_qk, w_vr, b_qk, b_vr, w_out, b_out, w1, b1, w2, b2,
          c_ident, c_identb, c_before, c_ones, c_route, c_tokens, out):
    ctx = ExitStack()
    with ctx:
        def sb(name, shape, dtype=F32):
            return ctx.enter_context(nc.sbuf_tensor(name, shape, dtype))

        def sem(name):
            return ctx.enter_context(nc.semaphore(name))

        q_parts = nc.dram_tensor("q_parts", (H, PARTS, D, S), BF16).ap()
        k_parts = nc.dram_tensor("k_parts", (H, PARTS, D, S), BF16).ap()

        xn_rows = nc.dram_tensor("xn_rows", (S, E), F32).ap()
        slot_tokens = nc.dram_tensor("slot_tokens", (SLOTS, 1), I32).ap()
        y_rows = nc.dram_tensor("y_rows", (SLOTS, E), F32).ap()

        x_sb = sb("x_sb", [P, TILES, E])
        wide = sb("wide", [P, TILES, E])
        big = sb("big", [P, KH * S])
        xn, attn_out = wide, wide
        xnT = big[:, :].rearrange("p (k s) -> p k s", k=KH)
        probs = big[:, :].rearrange("p (b q) -> p b q", q=QB)
        v_all = sb("v_all", [P, H, KT, D])
        v_flat = v_all[:, :, :, :].rearrange("p h k d -> p (h k d)")
        w1_sb = v_flat[:, 0:2 * KH * F].rearrange("p (b k f) -> p b k f", b=2, k=KH)
        w2_sb = v_flat[:, 2 * KH * F:2 * KH * F + 2 * FT * E].rearrange("p (b f e) -> p b f e", b=2, f=FT)
        hT = big[:, 0:2 * FT * RB].rearrange("p (b f r) -> p b f r", b=2, f=FT)
        at = 2 * FT * RB
        xg = big[:, at:at + 2 * RT * E].rearrange("p (b r e) -> p b r e", b=2, r=RT)
        at += 2 * RT * E
        xgT = big[:, at:at + 2 * KH * RB].rearrange("p (b k r) -> p b k r", b=2, k=KH)
        at += 2 * KH * RB
        y_sb = big[:, at:at + 2 * RT * E].rearrange("p (b r e) -> p b r e", b=2, r=RT)
        y_back = wide
        b1_all = sb("b1_all", [P, N_EXPERTS * FT])
        b1_sb = sb("b1_sb", [P, 2, FT])
        b2_sb = sb("b2_sb", [P, 2, E])
        before = sb("before", [P, P])
        ones = sb("ones", [P, P])
        route_c = sb("route_c", [P, N_EXPERTS * COUNT_STEPS + N_EXPERTS + BLOCKS])
        count_step = route_c[:, 0:N_EXPERTS * COUNT_STEPS].rearrange("p (e c) -> p e c", e=N_EXPERTS)
        first_wins = route_c[:, N_EXPERTS * COUNT_STEPS:N_EXPERTS * COUNT_STEPS + N_EXPERTS]
        block_no = route_c[:, N_EXPERTS * COUNT_STEPS + N_EXPERTS:]
        tokens = sb("tokens", [P, KT], I32)
        top = sb("top", [P, KT])
        one_hot = sb("one_hot", [P, KT, N_EXPERTS])
        ranks = sb("ranks", [P, 2, KT, N_EXPERTS])
        scan = sb("scan", [P, 2, KT, N_EXPERTS])
        over = sb("over", [P, N_EXPERTS, COUNT_STEPS])
        blocks = sb("blocks", [P, N_EXPERTS])
        block_end = sb("block_end", [P, 2, N_EXPERTS])
        block_cmp = sb("block_cmp", [P, BLOCKS, N_EXPERTS])
        block_sum = sb("block_sum", [P, BLOCKS])
        block_expert = sb("block_expert", [P, BLOCKS], I32)
        slots = sb("slots", [P, KT], I32)
        slot_now = sb("slot_now", [P, 1], I32)
        token_now = sb("token_now", [P, 1], I32)
        no_tokens = sb("no_tokens", [P, SLOTS // P], I32)
        slot_tok = sb("slot_tok", [P, SLOTS // P], I32)
        gather_now = sb("gather_now", [P, 2, RT], I32)
        keys = sb("keys", [P, KBUFS * S], BF16)
        q_max = sb("q_max", [P, 2, QB], BF16)
        q_exp = sb("q_exp", [P, 2, QB], BF16)
        v_unit = sb("v_unit", [P, 2, KT, VCOL])
        chunk_max = sb("chunk_max", [P, QT, NKC])
        neg_max = sb("neg_max", [P, 2, QT])
        rest = sb("rest", [P, 2, QT])
        max_parts = sb("max_parts", [P, PARTS * QT], BF16)
        max_rows = sb("max_rows", [PARTS * QT, 2, P], BF16)
        o_pairs = sb("o_pairs", [P, QT, 2, D + 1])
        o_sum = sb("o_sum", [P, QT, D + 1])
        inv_sum = sb("inv_sum", [P, QT])
        wqk_sb = sb("wqk_sb", [P, KH, 2 * E])
        wvr_sb = sb("wvr_sb", [P, KH, E + N_EXPERTS])
        wout_sb = sb("wout_sb", [P, KH, E])
        bqk_sb = sb("bqk_sb", [P, 4])
        bvr_sb = sb("bvr_sb", [P, E + N_EXPERTS])
        bout_sb = sb("bout_sb", [P, E])
        ident = sb("ident", [P, P])
        identb = sb("identb", [P, P], BF16)
        stats = sb("stats", [P, TILES, 6])
        mean_var = sb("mean_var", [P, TILES, 2])
        var_eps = sb("var_eps", [P, TILES])
        std = sb("std", [P, TILES])
        rstd = sb("rstd", [P, TILES])
        newton = sb("newton", [P, TILES])
        newton2 = sb("newton2", [P, TILES])
        qk_f32 = sb("qk_f32", [P, 2, 512])
        qk_rest = sb("qk_rest", [P, 2, 512])
        pv_sb = qk_rest[:, 0, :]
        o_cols = qk_f32[:, 0, :]
        qk_stage = sb("qk_stage", [P, 2, PARTS, 512], BF16)
        scores = sb("scores", [P, KT, N_EXPERTS])
        oT = sb("oT", [P, 2, KH, P])

        ring = ctx.enter_context(nc.psum_tensor("ring", [P, 2, 2, 512], F32))
        st = ctx.enter_context(nc.psum_tensor("st", [P, STBUFS, 512], F32))
        pv = ctx.enter_context(nc.psum_tensor("pv", [P, 512], F32))

        def bank(n):
            return ring[:, n // 2, n % 2, :]

        x_loaded = [sem(f"x_loaded{c}") for c in range(4)]
        w_loaded = sem("w_loaded")
        vec = sem("vec")
        var_ready = sem("var_ready")
        std_ready = sem("std_ready")
        xn_ready = sem("xn_ready")
        tr_ready = sem("tr_ready")
        tr_copied = sem("tr_copied")
        v_ready = sem("v_ready")
        v_copied = sem("v_copied")
        qk_ready = sem("qk_ready")
        qk_f32_ready = sem("qk_f32_ready")
        qk_copied = sem("qk_copied")
        rest_ready = sem("rest_ready")
        part2_ready = sem("part2_ready")
        part3_ready = sem("part3_ready")
        stored = [sem(f"stored{n}") for n in range(2)]
        sp_turns = sem("sp_turns")
        pool_turns = sem("pool_turns")
        k_first = sem("k_first")
        k_loaded = sem("k_loaded")
        qm_loaded = [sem(f"qm_loaded{n}") for n in range(2)]
        qe_loaded = [sem(f"qe_loaded{n}") for n in range(2)]
        ones_ready = sem("ones_ready")
        ring_full = sem("ring_full")
        ring_free = sem("ring_free")
        st_ready = sem("st_ready")
        exp_done = sem("exp_done")
        pv_done = sem("pv_done")
        pv_copied = sem("pv_copied")
        neg_ready = sem("neg_ready")
        pool_own = sem("pool_own")
        parts_ready = sem("parts_ready")
        inv_ready = sem("inv_ready")
        o_ready = sem("o_ready")
        aux_copied = sem("aux_copied")
        pairs_summed = sem("pairs_summed")
        out_scaled = sem("out_scaled")
        v_unit_ready = sem("v_unit_ready")
        bias_added = sem("bias_added")
        ot_ready = sem("ot_ready")
        ot_copied = sem("ot_copied")
        proj_ready = sem("proj_ready")
        proj_added = sem("proj_added")
        out_stored = sem("out_stored")
        xn_stored = sem("xn_stored")
        one_hot_ready = sem("one_hot_ready")
        ranks_ready = sem("ranks_ready")
        ranks_copied = sem("ranks_copied")
        slots_ready = sem("slots_ready")
        zeroed = sem("zeroed")
        slots_zeroed = sem("slots_zeroed")
        now_ready = sem("now_ready")
        scattered = sem("scattered")
        slot_tok_loaded = sem("slot_tok_loaded")
        w_ready = [sem(f"w_ready{n}") for n in range(2)]
        gather_ready = sem("gather_ready")
        gathered = [sem(f"gathered{n}") for n in range(2)]
        xgT_ready = sem("xgT_ready")
        xgT_copied = sem("xgT_copied")
        h_ready = sem("h_ready")
        gelu_done = sem("gelu_done")
        y_ready = sem("y_ready")
        y_copied = sem("y_copied")
        y_stored = [sem(f"y_stored{n}") for n in range(2)]
        y_back_ready = [sem(f"y_back_ready{c}") for c in range(4)]
        summed = sem("summed")

        xv = x.rearrange("(t p) e -> p t e", p=P)
        outv = out.rearrange("(t p) e -> p t e", p=P)
        CH = TILES // 4
        W_LOADS = 13
        W_BLOCK = 4 * DMA
        QK_LOADS = 3 * DMA
        QE_LOADS = 2 * QK_LOADS

        block = ctx.enter_context(nc.Block())

        @block.sync
        def _(sp):
            for c in range(4):
                sp.dma_start(x_sb[:, c * CH:(c + 1) * CH, :], xv[:, c * CH:(c + 1) * CH, :]).then_inc(x_loaded[c], 16)
            sp.dma_start(ident[:, :], c_ident).then_inc(w_loaded, 16)
            sp.dma_start(identb[:, :], c_identb).then_inc(w_loaded, 16)
            sp.dma_start(wvr_sb[:, :, :], w_vr.rearrange("(k p) n -> p k n", p=P)).then_inc(w_loaded, 16)
            sp.dma_start(bvr_sb[:, :], b_vr.partition_broadcast(P)).then_inc(w_loaded, 16)
            sp.dma_start(wqk_sb[:, :, :], w_qk.rearrange("(k p) n -> p k n", p=P)).then_inc(w_loaded, 16)
            sp.dma_start(bqk_sb[:, :], b_qk).then_inc(w_loaded, 16)
            sp.dma_start(wout_sb[:, :, :], w_out.rearrange("(k p) n -> p k n", p=P)).then_inc(w_loaded, 16)
            sp.dma_start(bout_sb[:, :], b_out.partition_broadcast(P)).then_inc(w_loaded, 16)
            sp.dma_start(before[:, :], c_before).then_inc(w_loaded, 16)
            sp.dma_start(ones[:, :], c_ones).then_inc(w_loaded, 16)
            sp.dma_start(route_c[:, :], c_route.partition_broadcast(P)).then_inc(w_loaded, 16)
            sp.dma_start(tokens[:, :], c_tokens).then_inc(w_loaded, 16)
            sp.dma_start(b1_all[:, :], b1).then_inc(w_loaded, 16)
            for c in range(4):
                sp.wait_ge(xn_ready, (c + 1) * CH)
                sp.dma_start(xn_rows.rearrange("(t p) e -> p t e", p=P)[:, c * CH:(c + 1) * CH, :],
                             xn[:, c * CH:(c + 1) * CH, :]).then_inc(xn_stored, 16)
            sp.wait_ge(zeroed, 1)
            sp.dma_start(slot_tokens.rearrange("(p c) o -> p (c o)", p=P), no_tokens[:, :]).then_inc(slots_zeroed, 16)

            def store_parts(nc_, mt):
                dst = (q_parts, q_parts, k_parts, k_parts)[mt]
                h0 = 8 * (mt % 2)
                wait_alone(sp, part3_ready, 4 * nc_ + mt + 1, sp_turns)
                for part in range(PARTS):
                    sp.dma_start(dst[h0:h0 + 8, part, :, bass.ds(nc_ * 512, 512)],
                                 qk_stage[:, mt % 2, part, :]).then_inc(stored[mt % 2], 16)

            with sp.Fori(0, S // 512) as nc_:
                for mt in range(4):
                    store_parts(nc_, mt)
            for n in range(2):
                wait(sp, stored[n], 16 * PARTS * 16)

            def load_keys(head, at, signal):
                for g, n, part in KEY_GROUPS:
                    sp.dma_start(keys[g * D:(g + n) * D, at:at + S],
                                 k_parts[head, part:part + n, :, :].rearrange("a d s -> (a d) s")).then_inc(signal, 16)

            def load_queries(unit, to, signal):
                src = q_parts[bass.ds((unit >> 3) & 15, 1), :, :, bass.ds((unit & 7) * QB, QB)]
                for g, n, part in QUERY_GROUPS:
                    one = src[:, part:part + 1, :, :].rearrange("h a d s -> (h a) d s")
                    sp.dma_start(to[g * D:(g + n) * D, :], one.to_broadcast([n, D, QB])).then_inc(signal, 16)

            load_keys(0, 0, k_first)
            load_queries(0, q_max[:, 0, :], qm_loaded[0])
            load_queries(1, q_max[:, 1, :], qm_loaded[1])
            load_keys(1, S, k_loaded)

            def step(i, t, keys_too=True, exp=True, ahead=True):
                s = 2 * i + t
                if keys_too:
                    wait_alone(sp, k_loaded, QK_LOADS + QK_LOADS * s, sp_turns)
                    wait_alone(sp, st_ready, KT * s, sp_turns)
                    eighth = (s & 7) * 512
                    slot = ((s >> 3) + 2) % KBUFS
                    for g, n, part in KEY_GROUPS:
                        sp.dma_start(keys[g * D:(g + n) * D, bass.ds(slot * S + eighth, 512)],
                                     k_parts[bass.ds(((s >> 3) + 2) & 15, 1), part:part + n, :, bass.ds(eighth, 512)]
                                     .rearrange("h a d s -> (h a d) s")).then_inc(k_loaded, 16)
                if exp:
                    wait_alone(sp, st_ready, KT * s, sp_turns)
                    load_queries(s + 1, q_exp[:, 1 - t, :], qe_loaded[1 - t])
                if ahead:
                    wait_alone(sp, ring_full, ring_base(s), sp_turns)
                    load_queries((s + 3) & 127, q_max[:, 1 - t, :], qm_loaded[1 - t])
                if exp:
                    wait(sp, aux_copied, s + 2)
                    for part in range(PARTS):
                        sp.dma_start(q_exp[SPLIT_ROWS + part:SPLIT_ROWS + part + 1, 1 - t, :]
                                     .rearrange("a (q c) -> a q c", q=QT),
                                     max_rows[part * QT:(part + 1) * QT, 1 - t, :]).then_inc(qe_loaded[1 - t], 16)

            wait(sp, ring_full, 16)
            load_queries(2, q_max[:, 0, :], qm_loaded[0])
            step(-1, 1, keys_too=False, ahead=False)
            step(0, 0)
            step(0, 1)
            with sp.Fori(1, TILES + 2) as i:
                step(i, 0)
                step(i, 1)
            sp.wait_ge(scattered, TILES * 16)
            sp.dma_start(slot_tok[:, :], slot_tokens.rearrange("(c p) o -> p (c o)", p=P),
                         allow_slow_non_contiguous=True).then_inc(slot_tok_loaded, 16)
            with sp.Fori(TILES + 2, 63) as i:
                step(i, 0)
                step(i, 1)
            step(63, 0, keys_too=False, ahead=False)
            wait(sp, k_loaded, QK_LOADS + QK_LOADS * 126)
            wait(sp, qm_loaded[0], QK_LOADS * 65)

            def load_expert(b, t):
                e = sp.value_load(block_expert[0:1, bass.ds(b, 1)], min_val=0, max_val=N_EXPERTS - 1)
                sp.dma_start(w1_sb[:, t, :, :], w1[bass.ds(e, 1), :, :, :].rearrange("x p k f -> (x p) k f")).then_inc(w_ready[t], 16)
                sp.dma_start(w2_sb[:, t, :, :], w2[bass.ds(e, 1), :, :, :].rearrange("x p f e -> (x p) f e")).then_inc(w_ready[t], 16)
                sp.dma_start(b1_sb[:, t, :], b1_all[:, bass.ds(e * FT, FT)]).then_inc(w_ready[t], 16)
                sp.dma_start(b2_sb[:, t, :], b2[bass.ds(e, 1), :].rearrange("x e -> (x e)").partition_broadcast(P)).then_inc(w_ready[t], 16)

            def expert_step(b, t, load=True):
                wait_alone(sp, y_copied, b + 1, sp_turns)
                sp.dma_start(y_rows[bass.ds(b * RB, RB), :].rearrange("(r p) e -> p r e", p=P), y_sb[:, t, :, :]).then_inc(y_stored[t], 16)
                if load:
                    load_expert(b + 2, t)

            sp.wait_ge(v_unit_ready, UNITS)
            load_expert(0, 0)
            load_expert(1, 1)
            with sp.Fori(0, (BLOCKS - 3) // 2) as i:
                expert_step(2 * i, 0)
                expert_step(2 * i + 1, 1)
            expert_step(BLOCKS - 3, 0)
            expert_step(BLOCKS - 2, 1, load=False)
            expert_step(BLOCKS - 1, 0, load=False)

            for c in range(4):
                wait(sp, summed, (c + 1) * CH)
                sp.dma_start(outv[:, c * CH:(c + 1) * CH, :], x_sb[:, c * CH:(c + 1) * CH, :]).then_inc(out_stored, 16)
            sp.wait_ge(out_stored, 64)

        @block.tensor
        def _(pe):
            pe.wait_ge(w_loaded, W_LOADS * 16)

            def value_tile(kt):
                wait(pe, tr_copied, kt // 2 + 1)
                wait(pe, v_copied, kt - 2)
                for k in range(KH):
                    last = nc.tensor.matmul(st[:, kt % STBUFS, 0:E + N_EXPERTS], xnT[:, k, kt * P:(kt + 1) * P],
                                            wvr_sb[:, k, :], start=(k == 0), stop=(k == KH - 1))
                last.then_inc(v_ready, 1)

            for n in range(TILES // 2):
                pe.wait_ge(xn_ready, 2 * n + 2)
                wait(pe, tr_copied, n - 3)
                for k in range(KH):
                    for u in range(2):
                        last = nc.tensor.transpose(bank(n % 4)[:, (2 * k + u) * P:(2 * k + u + 1) * P],
                                                   xn[:, 2 * n + u, k * P:(k + 1) * P], ident[:, :])
                last.then_inc(tr_ready, 1)
                if n:
                    value_tile(2 * n - 2)
                    value_tile(2 * n - 1)
            value_tile(TILES - 2)
            value_tile(TILES - 1)

            def qk_item(c, mt):
                wait(pe, qk_copied, 4 * c + mt - 3)
                for k in range(KH):
                    last = nc.tensor.matmul(bank(mt), wqk_sb[:, k, mt * P:(mt + 1) * P],
                                            xnT[:, k, bass.ds(c * 512, 512)], start=(k == 0), stop=(k == KH - 1))
                last.then_inc(qk_ready, 1)

            for mt in range(4):
                qk_item(0, mt)
            with pe.Fori(1, S // 512) as c:
                for mt in range(4):
                    qk_item(c, mt)
            pe.wait_ge(qk_copied, 32)
            pe.wait_ge(v_copied, 32)
            pe.wait_ge(ones_ready, 3)

            pe.wait_ge(one_hot_ready, 1)
            oh = one_hot[:, :, :].rearrange("p t e -> p (t e)")
            nc.tensor.matmul(pv[:, 0:KT * N_EXPERTS], before[:, :], oh, start=True, stop=True)
            nc.tensor.matmul(pv[:, KT * N_EXPERTS:], ones[:, :], oh, start=True, stop=True).then_inc(ranks_ready, 1)

            def max_chunk(s, t, c, par, key0):
                if c == CHUNKS // 2 + 1:
                    wait(pe, aux_copied, s + 2)
                else:
                    wait(pe, ring_free, CHUNKS * (s + 2) + c - (1 if c != CHUNKS // 2 else 0))
                qt, kc = c // NKC, c % NKC
                for half in range(2):
                    last = nc.tensor.matmul(ring[:, par, half, :], q_max[0:SPLIT_ROWS, t, qt * P:(qt + 1) * P],
                                            keys[0:SPLIT_ROWS, bass.ds(key0 + kc * KCHUNK + half * 512, 512)],
                                            start=True, stop=True)
                last.then_inc(ring_full, 1)

            def aux(s, par, maxima, sums):
                wait(pe, ring_free, CHUNKS * (s + 2) + CHUNKS // 2 - 1 if not (isinstance(s, int) and s > 125) else CHUNKS * UNITS)
                wait(pe, aux_copied, s if isinstance(s, int) and s == UNITS else 0)
                if sums:
                    wait(pe, pv_copied, s)
                    for qt in range(QT):
                        last = nc.tensor.transpose(ring[:, par, 0, qt * P:(qt + 1) * P],
                                                   pv_sb[:, qt * P:(qt + 1) * P], ident[:, :])
                if maxima:
                    wait(pe, parts_ready, s + 2)
                    last = nc.tensor.transpose(ring[:, par, 1, :].bitcast(BF16)[0:PARTS * QT, 0:P],
                                               max_parts[:, :], identb[:, :])
                last.then_inc(ring_full, 1)

            def pv_batch(s, t, b):
                wait(pe, exp_done, KT * s + BATCH * (b + 1))
                if b == 0:
                    wait(pe, ranks_copied, 1)
                    wait(pe, pv_copied, s)
                    wait(pe, v_unit_ready, s + 1)
                for j in range(BATCH * b, BATCH * (b + 1)):
                    c = 32 * (j % 4)
                    last = nc.tensor.matmul(pv[c:c + VCOL, :], v_unit[:, t, j, :], probs[:, j % PBUFS, :],
                                            start=(j < 4), stop=(j >= KT - 4))
                last.then_inc(pv_done, 1)

            def step(i, t, maxima=True, exp=True, prev=True, aux_max=True, aux_sum=True, base=None):
                s = 2 * i + t
                base = ring_base(s) if base is None else base
                has_aux = aux_max or aux_sum
                if maxima:
                    wait(pe, qm_loaded[t], QK_LOADS * (i + 2))
                    wait(pe, k_first, QK_LOADS)
                    wait(pe, k_loaded, QK_LOADS if isinstance(s, int) and s < 2 else QK_LOADS * s)
                    max_keys = (((s + 2) >> 3) % KBUFS) * S
                if exp:
                    exp_keys = ((s >> 3) % KBUFS) * S
                    wait(pe, qe_loaded[t], QE_LOADS * (i + 1))
                k = 0
                first = (base % 2) if isinstance(base, int) else (1 + t) % 2
                for j in range(KT):
                    if exp:
                        if j == 0:
                            wait(pe, exp_done, KT * s - 1)
                        elif j == 1:
                            wait(pe, exp_done, KT * s)
                        elif j > 2:
                            wait(pe, exp_done, KT * s + j - 2)
                        nc.tensor.matmul(st[:, j % STBUFS, :], keys[0:SHIFT_ROWS, bass.ds(exp_keys + j * P, P)],
                                         q_exp[0:SHIFT_ROWS, t, :], start=True, stop=True).then_inc(st_ready, 1)
                    if maxima and j % 2 == 1:
                        max_chunk(s, t, j // 2, (first + k) % 2, max_keys)
                        k += 1
                    if j % BATCH == PV_LAG % BATCH:
                        b = (j - PV_LAG) // BATCH - 1
                        if b >= 0 and exp:
                            pv_batch(s, t, b)
                        if b < 0 and prev:
                            pv_batch(s - 1, 1 - t, NBATCH + b)
                    if j == CHUNKS and has_aux:
                        aux(s, (first + k) % 2, aux_max, aux_sum)
                        k += 1

            step(-1, 0, exp=False, prev=False, aux_max=False, aux_sum=False)
            step(-1, 1, exp=False, prev=False, aux_sum=False)
            step(0, 0, prev=False, aux_sum=False)
            step(0, 1)
            with pe.Fori(1, 63) as i:
                step(i, 0)
                step(i, 1)
            END = ring_base(126)
            step(63, 0, maxima=False)
            step(63, 1, maxima=False, aux_max=False, base=END + 1)
            for b in range(NBATCH - LATE, NBATCH):
                pv_batch(127, 1, b)
            aux(128, END % 2, False, True)

            def project(n):
                wait(pe, ot_copied, n + 1)
                wait(pe, proj_added, n - 1)
                for k in range(KH):
                    last = nc.tensor.matmul(bank(2 + n % 2)[:, 0:E], oT[:, n % 2, k, :], wout_sb[:, k, :],
                                            start=(k == 0), stop=(k == KH - 1))
                last.then_inc(proj_ready, 1)

            for n in range(TILES):
                wait(pe, ot_copied, n - 1)
                if n == 0:
                    pe.wait_ge(out_scaled, UNITS)
                for k in range(KH):
                    last = nc.tensor.transpose(bank(n % 2)[:, k * P:(k + 1) * P], attn_out[:, n, k * P:(k + 1) * P], ident[:, :])
                last.then_inc(ot_ready, 1)
                if n:
                    project(n - 1)
            project(TILES - 1)

            def turn_block(b, t, i):
                wait(pe, gathered[t], RT * DMA * (i + 1))
                wait(pe, xgT_copied, b)
                for k in range(KH):
                    for r in range(RT):
                        last = nc.tensor.transpose(st[:, 0, (k * RT + r) * P:(k * RT + r + 1) * P],
                                                   xg[:, t, r, k * P:(k + 1) * P], ident[:, :])
                last.then_inc(xgT_ready, 1)

            def hidden(b, t, i):
                wait(pe, xgT_copied, b + 1)
                wait(pe, w_ready[t], W_BLOCK * (i + 1))
                for f in range(FT):
                    if f % 2 == 0:
                        wait(pe, gelu_done, (FT // 2) * (b - 1) + f // 2 + 1)
                    for k in range(KH):
                        last = nc.tensor.matmul(bank(f // 2)[:, (f % 2) * RB:(f % 2 + 1) * RB], w1_sb[:, t, k, f * P:(f + 1) * P],
                                                xgT[:, t, k, :], start=(k == 0), stop=(k == KH - 1))
                    if f % 2:
                        last.then_inc(h_ready, 1)

            def output(b, t):
                wait(pe, gelu_done, (FT // 2) * (b + 1))
                wait(pe, y_copied, b - 1)
                for r in range(RT):
                    for f in range(FT):
                        last = nc.tensor.matmul(st[:, 1 + t, r * E:(r + 1) * E], hT[:, t, f, r * P:(r + 1) * P],
                                                w2_sb[:, t, f, :], start=(f == 0), stop=(f == FT - 1))
                last.then_inc(y_ready, 1)

            def expert_step(i, t, ahead=True):
                b = 2 * i + t
                hidden(b, t, i)
                if ahead:
                    turn_block(b + 1, 1 - t, i + t)
                output(b, t)

            pe.wait_ge(proj_added, TILES)
            turn_block(0, 0, 0)
            expert_step(0, 0)
            expert_step(0, 1)
            with pe.Fori(1, BLOCKS // 2) as i:
                expert_step(i, 0)
                expert_step(i, 1)
            expert_step(BLOCKS // 2, 0, ahead=False)

        @block.scalar
        def _(act):
            for c in range(4):
                act.wait_ge(var_ready, c + 1)
                nc.scalar.activation(std[:, c * CH:(c + 1) * CH], var_eps[:, c * CH:(c + 1) * CH], ACT.Sqrt).then_inc(std_ready, 1)
            for n in range(TILES // 2):
                act.wait_ge(tr_ready, n + 1)
                nc.scalar.activation(xnT[:, :, n * 2 * P:(n + 1) * 2 * P],
                                     bank(n % 4).rearrange("p (k s) -> p k s", k=KH), ACT.Copy).then_inc(tr_copied, 1)

            def qk_item(c, mt):
                n = 4 * c + mt
                wait(act, qk_ready, n + 1)
                wait(act, rest_ready, n - 1)
                nc.scalar.activation(qk_f32[:, mt % 2, :], bank(mt), ACT.Identity, bias=bqk_sb[:, mt:mt + 1]).then_inc(qk_f32_ready, 1)
                wait(act, stored[mt % 2], 16 * PARTS * (2 * c + mt // 2))
                nc.scalar.activation(qk_stage[:, mt % 2, 0, :], bank(mt), ACT.Identity, bias=bqk_sb[:, mt:mt + 1]).then_inc(qk_copied, 1)

            act.wait_ge(w_loaded, W_LOADS * 16)
            for mt in range(4):
                qk_item(0, mt)
            with act.Fori(1, S // 512) as c:
                for mt in range(4):
                    qk_item(c, mt)

            def copy_pv(s):
                wait(act, pv_done, NBATCH * s)
                if not (isinstance(s, int) and s < 2):
                    wait(act, ring_full, ring_base(s) - 8 if not (isinstance(s, int) and s > 126) else ring_base(126) + s - 126)
                nc.scalar.activation(pv_sb, pv[:, :], ACT.Copy).then_inc(pv_copied, 1)

            def aux(s, t, n, maxima, sums):
                wait(act, ring_full, n + 1)
                if maxima:
                    wait(act, qe_loaded[1 - t], QE_LOADS * ((s + 1) >> 1))
                    last = nc.scalar.activation(max_rows[:, 1 - t, :], aux_bank(n)[1].bitcast(BF16)[0:PARTS * QT, 0:P], ACT.Copy)
                if sums:
                    wait(act, pairs_summed, s - 1)
                    last = nc.scalar.activation(o_cols, aux_bank(n)[0], ACT.Copy)
                last.then_inc(aux_copied, 1)

            def aux_bank(n):
                par = n % 2 if isinstance(n, int) else aux_par[0]
                return ring[:, par, 0, :], ring[:, par, 1, :]

            aux_par = [0]

            def step(i, t, prev=True, aux_max=True, aux_sum=True, aux_n=None):
                s = 2 * i + t
                for j in range(KT):
                    if j == CHUNKS + 1:
                        aux_par[0] = (1 + t + CHUNKS // 2) % 2
                        aux(s, t, ring_base(s) + CHUNKS // 2 if aux_n is None else aux_n, aux_max, aux_sum)
                    wait(act, st_ready, KT * s + j + 1)
                    wait(act, pv_done, NBATCH * s + j // BATCH + 1 - PBUFS // BATCH)
                    nc.scalar.activation(probs[:, j % PBUFS, :], st[:, j % STBUFS, :], ACT.Exp, scale=0.25).then_inc(exp_done, 1)
                    if j == PV_LAG + 1 and prev:
                        copy_pv(s)

            END = ring_base(126)
            aux(-1, 1, ring_base(-1) + CHUNKS // 2, True, False)
            step(0, 0, prev=False, aux_sum=False)
            step(0, 1)
            with act.Fori(1, 63) as i:
                step(i, 0)
                step(i, 1)
            step(63, 0, aux_n=END)
            step(63, 1, aux_max=False, aux_n=END + 1)
            copy_pv(128)
            aux(128, 0, END + 2, False, True)

            for n in range(TILES):
                act.wait_ge(ot_ready, n + 1)
                wait(act, proj_ready, n - 1)
                nc.scalar.activation(oT[:, n % 2, :, :].rearrange("p k s -> p (k s)"), bank(n % 2)[:, 0:KH * P], ACT.Copy).then_inc(ot_copied, 1)

            def expert_step(i, t):
                b = 2 * i + t
                wait(act, w_ready[t], W_BLOCK * (i + 1))
                wait(act, y_ready, b - 1)
                for f in range(FT):
                    if f % 2 == 0:
                        wait(act, h_ready, (FT // 2) * b + f // 2 + 1)
                    ins = nc.scalar.activation(hT[:, t, f, :], bank(f // 2)[:, (f % 2) * RB:(f % 2 + 1) * RB],
                                               ACT.Gelu, bias=b1_sb[:, t, f:f + 1])
                    if f % 2:
                        ins.then_inc(gelu_done, 1)

            expert_step(0, 0)
            expert_step(0, 1)
            with act.Fori(1, BLOCKS // 2) as i:
                expert_step(i, 0)
                expert_step(i, 1)
            expert_step(BLOCKS // 2, 0)

        @block.vector
        def _(dve):
            count = [0]

            def chained(ins):
                count[0] += 1
                ins.then_inc(vec, 1)
                dve.wait_ge(vec, count[0])

            def normalise(c):
                lo, hi = c * CH, (c + 1) * CH
                dve.wait_ge(std_ready, c + 1)
                chained(nc.vector.reciprocal(rstd[:, lo:hi], std[:, lo:hi]))
                chained(nc.vector.tensor_tensor(newton[:, lo:hi], rstd[:, lo:hi], rstd[:, lo:hi], ALU.mult))
                chained(nc.vector.tensor_tensor(newton2[:, lo:hi], newton[:, lo:hi], var_eps[:, lo:hi], ALU.mult))
                chained(nc.vector.tensor_scalar(newton[:, lo:hi], newton2[:, lo:hi], -0.5, 1.5, ALU.mult, ALU.add))
                chained(nc.vector.tensor_tensor(std[:, lo:hi], rstd[:, lo:hi], newton[:, lo:hi], ALU.mult))
                for n in range(lo, hi):
                    nc.vector.tensor_scalar(xn[:, n, :], x_sb[:, n, :], mean_var[:, n, 0:1], std[:, n:n + 1],
                                            ALU.subtract, ALU.mult).then_inc(xn_ready, 1)

            for c in range(4):
                lo, hi = c * CH, (c + 1) * CH
                dve.wait_ge(x_loaded[c], 16)
                for n in range(lo, hi):
                    ins = nc.vector.bn_stats(stats[:, n, :], x_sb[:, n, :])
                    ins.then_inc(vec, 1)
                    count[0] += 1
                dve.wait_ge(vec, count[0])
                for n in range(lo, hi):
                    ins = nc.vector.bn_aggr(mean_var[:, n, :], stats[:, n, :])
                    ins.then_inc(vec, 1)
                    count[0] += 1
                dve.wait_ge(vec, count[0])
                nc.vector.tensor_scalar(var_eps[:, lo:hi], mean_var[:, lo:hi, 1], EPS, None, ALU.add).then_inc(var_ready, 1)
                if c:
                    normalise(c - 1)
            normalise(3)

            dve.wait_ge(w_loaded, W_LOADS * 16)
            for kt in range(TILES):
                dve.wait_ge(v_ready, kt + 1)
                b = st[:, kt % STBUFS, :]
                nc.vector.tensor_tensor(v_all[:, :, kt, :], b[:, 0:E].rearrange("p (h d) -> p h d", h=H),
                                        bvr_sb[:, 0:E].rearrange("p (h d) -> p h d", h=H), ALU.add)
                nc.vector.tensor_tensor(scores[:, kt, :], b[:, E:E + N_EXPERTS], bvr_sb[:, E:E + N_EXPERTS], ALU.add).then_inc(v_copied, 1)

            def over_experts(a):
                return a.unsqueeze(2).to_broadcast([P, a.shape[1], N_EXPERTS])

            def over_rows(a, n):
                return a.unsqueeze(1).to_broadcast([P, n, N_EXPERTS])

            dve.wait_ge(v_copied, TILES)
            chained(nc.vector.tensor_reduce(top[:, :], scores[:, :, :], axis=X_AXIS, op=ALU.max))
            chained(nc.vector.tensor_tensor(scan[:, 0, :, :], scores[:, :, :], over_experts(top[:, :]), ALU.is_equal))
            chained(nc.vector.tensor_tensor(scan[:, 1, :, :], scan[:, 0, :, :], over_rows(first_wins, KT), ALU.mult))
            chained(nc.vector.tensor_reduce(top[:, :], scan[:, 1, :, :], axis=X_AXIS, op=ALU.max))
            nc.vector.tensor_tensor(one_hot[:, :, :], over_rows(first_wins, KT), over_experts(top[:, :]), ALU.is_equal).then_inc(one_hot_ready, 1)

            def qk_item(c, mt):
                n = 4 * c + mt
                wait(dve, qk_f32_ready, n + 1)
                wait(dve, qk_copied, n + 1)
                wait(dve, part3_ready, n - 1)
                nc.vector.tensor_tensor(qk_rest[:, mt % 2, :], qk_f32[:, mt % 2, :], qk_stage[:, mt % 2, 0, :], ALU.subtract).then_inc(rest_ready, 1)
                wait(dve, rest_ready, n + 1)
                nc.vector.tensor_copy(qk_stage[:, mt % 2, 1, :], qk_rest[:, mt % 2, :]).then_inc(part2_ready, 1)

            for mt in range(4):
                qk_item(0, mt)
            with dve.Fori(1, S // 512) as c:
                for mt in range(4):
                    qk_item(c, mt)

            def max_chunk(c, n, par):
                wait(dve, ring_full, n + 1)
                nc.vector.tensor_reduce(chunk_max[:, c // NKC, c % NKC:c % NKC + 1], ring[:, par, :, :].rearrange("p a b -> p (a b)"),
                                        axis=X_AXIS, op=ALU.max).then_inc(ring_free, 1)

            def invert(s):
                wait(dve, o_ready, s)
                nc.vector.reciprocal(inv_sum[:, :], o_sum[:, :, D]).then_inc(inv_ready, 1)

            def step(i, t, aux_max=True, aux_sum=True):
                s = 2 * i + t
                base = ring_base(s)
                first = (base % 2) if isinstance(base, int) else (1 + t) % 2
                k = 0
                wait(dve, neg_ready, s + 2)
                for c in range(CHUNKS):
                    if c == CHUNKS // 2 and (aux_max or aux_sum):
                        k += 1
                    if c == CHUNKS - 2 and aux_sum:
                        invert(s)
                    max_chunk(c, base + k, (first + k) % 2)
                    k += 1
                wait(dve, ring_free, CHUNKS * (s + 3))
                nc.vector.tensor_reduce(neg_max[:, t, :], chunk_max[:, :, :], axis=X_AXIS, op=ALU.max, negate=True).then_inc(neg_ready, 1)

            def route():
                rank, total = ranks[:, 0, :, :], ranks[:, 1, :, :]
                src = total
                for n, shift in enumerate((1, 2, 4, 8, 16)):
                    dst = scan[:, n % 2, :, :]
                    chained(nc.vector.tensor_copy(dst[:, 0:shift, :], src[:, 0:shift, :]))
                    chained(nc.vector.tensor_tensor(dst[:, shift:, :], src[:, shift:, :], src[:, 0:KT - shift, :], ALU.add))
                    src = dst
                counts = src[:, KT - 1, :]
                chained(nc.vector.tensor_tensor(over[:, :, :], counts.unsqueeze(2).to_broadcast([P, N_EXPERTS, COUNT_STEPS]), count_step, ALU.is_gt))
                chained(nc.vector.tensor_reduce(blocks[:, :], over[:, :, :], axis=X_AXIS, op=ALU.add))
                bsrc = blocks[:, :]
                for n, shift in enumerate((1, 2, 4)):
                    bdst = block_end[:, n % 2, :]
                    chained(nc.vector.tensor_copy(bdst[:, 0:shift], bsrc[:, 0:shift]))
                    chained(nc.vector.tensor_tensor(bdst[:, shift:], bsrc[:, shift:], bsrc[:, 0:N_EXPERTS - shift], ALU.add))
                    bsrc = bdst
                chained(nc.vector.tensor_tensor(block_cmp[:, :, :], over_experts(block_no), over_rows(bsrc, BLOCKS), ALU.is_ge))
                chained(nc.vector.tensor_reduce(block_sum[:, :], block_cmp[:, :, :], axis=X_AXIS, op=ALU.add))
                chained(nc.vector.tensor_scalar(block_expert[:, :], block_sum[:, :], float(N_EXPERTS - 1), None, ALU.min))
                other = scan[:, 1, :, :]
                chained(nc.vector.tensor_tensor(blocks[:, :], bsrc, blocks[:, :], ALU.subtract))
                chained(nc.vector.tensor_scalar(blocks[:, :], blocks[:, :], float(RB), None, ALU.mult))
                chained(nc.vector.tensor_tensor(other, src, total, ALU.subtract))
                chained(nc.vector.tensor_tensor(other, other, rank, ALU.add))
                chained(nc.vector.tensor_tensor(other, other, over_rows(blocks[:, :], KT), ALU.add))
                chained(nc.vector.tensor_tensor(other, other, one_hot[:, :, :], ALU.mult))
                chained(nc.vector.tensor_reduce(top[:, :], other, axis=X_AXIS, op=ALU.add))
                nc.vector.tensor_copy(slots[:, :], top[:, :]).then_inc(slots_ready, 1)

            dve.wait_ge(ranks_ready, 1)
            nc.vector.tensor_copy(ranks[:, :, :, :].rearrange("p a t e -> p (a t e)"), pv[:, :]).then_inc(ranks_copied, 1)
            step(-1, 0, aux_max=False, aux_sum=False)
            step(-1, 1, aux_sum=False)
            step(0, 0, aux_sum=False)
            step(0, 1)
            dve.wait_ge(ranks_copied, 1)
            route()
            with dve.Fori(1, 63) as i:
                step(i, 0)
                step(i, 1)
            for s in (126, 127, 128):
                invert(s)

            dve.wait_ge(bias_added, TILES)
            for n in range(TILES):
                dve.wait_ge(proj_ready, n + 1)
                nc.vector.tensor_tensor(x_sb[:, n, :], bank(2 + n % 2)[:, 0:E], x_sb[:, n, :], ALU.add).then_inc(proj_added, 1)

            def turned(b, t):
                wait(dve, xgT_ready, b + 1)
                wait(dve, h_ready, (FT // 2) * (b - 1))
                nc.vector.tensor_copy(xgT[:, t, :, :].rearrange("p k r -> p (k r)"), st[:, 0, :]).then_inc(xgT_copied, 1)

            def expert_step(i, t, ahead=True):
                b = 2 * i + t
                if ahead:
                    turned(b + 1, 1 - t)
                wait(dve, y_stored[t], DMA * i)
                wait(dve, w_ready[t], W_BLOCK * (i + 1))
                wait(dve, y_ready, b + 1)
                nc.vector.tensor_tensor(y_sb[:, t, :, :], st[:, 1 + t, :].rearrange("p (r e) -> p r e", r=RT),
                                        b2_sb[:, t, :].unsqueeze(1).to_broadcast([P, RT, E]), ALU.add).then_inc(y_copied, 1)

            turned(0, 0)
            expert_step(0, 0)
            expert_step(0, 1)
            with dve.Fori(1, BLOCKS // 2) as i:
                expert_step(i, 0)
                expert_step(i, 1)
            expert_step(BLOCKS // 2, 0, ahead=False)
            for n in range(TILES):
                dve.wait_ge(y_back_ready[n // CH], 16 * CH)
                nc.vector.tensor_tensor(x_sb[:, n, :], x_sb[:, n, :], y_back[:, n, :], ALU.add).then_inc(summed, 1)

        @block.gpsimd
        def _(pool):
            nc.gpsimd.memset(no_tokens[:, :], 0).then_inc(zeroed, 1)
            pool.wait_ge(zeroed, 1)
            nc.gpsimd.memset(keys[SPLIT_ROWS:SHIFT_ROWS, :], 1.0).then_inc(ones_ready, 1)
            pool.wait_ge(ones_ready, 1)
            nc.gpsimd.memset(v_unit[:, :, :, D:D + 1], 1.0).then_inc(ones_ready, 1)
            pool.wait_ge(ones_ready, 2)
            nc.gpsimd.memset(v_unit[:, :, :, D + 1:VCOL], 0.0).then_inc(ones_ready, 1)

            def qk_item(c, mt):
                n = 4 * c + mt
                wait(pool, part2_ready, n + 1)
                nc.gpsimd.tensor_tensor(qk_stage[:, mt % 2, 2, :], qk_rest[:, mt % 2, :], qk_stage[:, mt % 2, 1, :], ALU.subtract).then_inc(part3_ready, 1)

            with pool.Fori(0, S // 512) as c:
                for mt in range(4):
                    qk_item(c, mt)
            pool.wait_ge(xn_ready, TILES)
            pool.wait_ge(w_loaded, W_LOADS * 16)

            def values(u, to):
                wait_alone(pool, pv_done, NBATCH * (u - 1), pool_turns)
                nc.gpsimd.tensor_copy(v_unit[:, to, :, 0:D], v_all[:, bass.ds((u >> 3) & 15, 1), :, :].rearrange("p h k d -> p (h k) d")).then_inc(v_unit_ready, 1)

            def step(i, t, sums=True):
                u = 2 * i + t + 1
                wait_alone(pool, neg_ready, u + 1, pool_turns)
                nm = neg_max[:, 1 - t, :]
                p = [max_parts[:, n * QT:(n + 1) * QT] for n in range(PARTS)]
                nc.gpsimd.tensor_copy(p[0], nm).then_inc(pool_own, 1)
                wait(pool, pool_own, 3 * u + 1)
                nc.gpsimd.tensor_tensor(rest[:, 0, :], nm, p[0], ALU.subtract).then_inc(pool_own, 1)
                wait_alone(pool, pool_own, 3 * u + 2, pool_turns)
                nc.gpsimd.tensor_copy(p[1], rest[:, 0, :]).then_inc(pool_own, 1)
                wait(pool, pool_own, 3 * u + 3)
                nc.gpsimd.tensor_tensor(p[2], rest[:, 0, :], p[1], ALU.subtract).then_inc(parts_ready, 1)
                values(u, 1 - t)
                if sums:
                    scale(u - 1)

            def scale(s):
                o = o_cols.rearrange("p (q g v) -> p q g v", q=QT, g=P // VCOL)[:, :, :, 0:D + 1]
                wait(pool, aux_copied, s + 2)
                nc.gpsimd.tensor_tensor(o_pairs[:, :, :, :], o[:, :, 0:2, :], o[:, :, 2:4, :], ALU.add).then_inc(pairs_summed, 1)
                wait(pool, pairs_summed, s)
                nc.gpsimd.tensor_tensor(o_sum[:, :, :], o_pairs[:, :, 0, :], o_pairs[:, :, 1, :], ALU.add).then_inc(o_ready, 1)
                if isinstance(s, int) and s == 1:
                    pool.wait_ge(xn_stored, 4 * 16)
                wait_alone(pool, inv_ready, s, pool_turns)
                u = s - 1
                nc.gpsimd.tensor_tensor(attn_out[:, bass.ds((u & 7) * QT, QT), bass.ds(((u >> 3) & 15) * D, D)],
                                        o_sum[:, :, 0:D], inv_sum[:, :].unsqueeze(2).to_broadcast([P, QT, D]), ALU.mult).then_inc(out_scaled, 1)

            pool.wait_ge(v_copied, TILES)
            step(-1, 1, sums=False)
            step(0, 0, sums=False)
            step(0, 1)
            pool.wait_ge(slots_ready, 1)
            pool.wait_ge(slots_zeroed, 16)
            with pool.Fori(1, TILES + 1) as i:
                step(i, 0)
                step(i, 1)
                wait_alone(pool, scattered, DMA * (i - 1), pool_turns)
                nc.gpsimd.tensor_copy(slot_now[:, :], slots[:, bass.ds(i - 1, 1)]).then_inc(now_ready, 1)
                nc.gpsimd.tensor_copy(token_now[:, :], tokens[:, bass.ds(i - 1, 1)]).then_inc(now_ready, 1)
                wait_alone(pool, now_ready, 2 * i, pool_turns)
                nc.gpsimd.indirect_dma_start(out=slot_tokens, out_offset=bass.IndirectOffsetOnAxis(ap=slot_now[:, :], axis=0),
                                             in_=token_now[:, :], in_offset=None).then_inc(scattered, 16)
                tile_n = x_sb[:, bass.ds(i - 1, 1), :].rearrange("p n e -> p (n e)")
                nc.gpsimd.tensor_tensor(tile_n, tile_n, bout_sb[:, :], ALU.add).then_inc(bias_added, 1)
            with pool.Fori(TILES + 1, 63) as i:
                step(i, 0)
                step(i, 1)
            step(63, 0)
            scale(127)
            scale(128)

            def gather(i, t):
                b = 2 * i + t
                wait_alone(pool, xgT_ready, b - 1, pool_turns)
                wait_alone(pool, gathered[t], RT * DMA * i, pool_turns)
                nc.gpsimd.tensor_copy(gather_now[:, t, :], slot_tok[:, bass.ds(b * RT, RT)]).then_inc(gather_ready, 1)
                wait_alone(pool, gather_ready, b + 1, pool_turns)
                for r in range(RT):
                    nc.gpsimd.indirect_dma_start(out=xg[:, t, r, :], out_offset=None, in_=xn_rows,
                                                 in_offset=bass.IndirectOffsetOnAxis(ap=gather_now[:, t, r:r + 1], axis=0)).then_inc(gathered[t], 16)

            pool.wait_ge(slot_tok_loaded, 16)
            pool.wait_ge(pv_done, NBATCH * UNITS)
            gather(0, 0)
            gather(0, 1)
            with pool.Fori(1, BLOCKS // 2) as i:
                gather(i, 0)
                gather(i, 1)
            gather(BLOCKS // 2, 0)
            pool.wait_ge(y_stored[0], DMA * (BLOCKS // 2 + 1))
            pool.wait_ge(y_stored[1], DMA * (BLOCKS // 2))
            for n in range(TILES):
                nc.gpsimd.indirect_dma_start(out=y_back[:, n, :], out_offset=None, in_=y_rows,
                                             in_offset=bass.IndirectOffsetOnAxis(ap=slots[:, n:n + 1], axis=0)).then_inc(y_back_ready[n // CH], 16)


def kernel(**inputs):
    import numpy as np
    import concourse.bacc as bacc
    from concourse.bass_utils import run_bass_kernel_spmd

    a = {n: np.asarray(v) for n, v in inputs.items()}
    wqkv = a["L0_attn_Wqkv"].reshape(E, H, 3, D)
    bqkv = a["L0_attn_bqkv"].reshape(H, 3, D)
    import ml_dtypes
    arrays = {
        "x": a["L0_attn_x"].reshape(S, E),
        "w_qk": np.concatenate([wqkv[:, :, n, :].reshape(E, E) for n in (0, 1)], axis=1),
        "w_vr": np.concatenate([wqkv[:, :, 2, :].reshape(E, E), a["L0_ffn_wr"]], axis=1),
        "b_qk": np.ascontiguousarray(np.concatenate([bqkv[:, n, :].reshape(E) for n in (0, 1)]).reshape(4, P).T),
        "b_vr": np.concatenate([bqkv[:, 2, :].reshape(E), a["L0_ffn_br"]]),
        "w_out": a["L0_attn_Wout"],
        "b_out": a["L0_attn_bout"],
        "w1": a["L0_ffn_w1"].reshape(N_EXPERTS, KH, P, F).transpose(0, 2, 1, 3),
        "b1": a["L0_ffn_b1"].reshape(N_EXPERTS * FT, P).T,
        "w2": a["L0_ffn_w2"].reshape(N_EXPERTS, FT, P, E).transpose(0, 2, 1, 3),
        "b2": a["L0_ffn_b2"],
        "c_ident": np.eye(P, dtype=np.float32),
        "c_identb": np.eye(P, dtype=ml_dtypes.bfloat16),
        "c_before": np.triu(np.ones((P, P), np.float32), 1),
        "c_ones": np.ones((P, P), np.float32),
        "c_route": np.concatenate([np.tile(RB * np.arange(COUNT_STEPS), N_EXPERTS), N_EXPERTS - np.arange(N_EXPERTS),
                                   np.arange(BLOCKS)]).astype(np.float32),
        "c_tokens": np.arange(S, dtype=np.int32).reshape(TILES, P).T,
    }
    arrays = {n: np.ascontiguousarray(v) for n, v in arrays.items()}
    nc = bacc.Bacc("TRN2", target_bir_lowering=False, num_devices=1)
    args = [nc.dram_tensor(n, v.shape, mybir.dt.from_np(v.dtype), kind="ExternalInput").ap() for n, v in arrays.items()]
    out = nc.dram_tensor("out", (S, E), F32, kind="ExternalOutput").ap()
    build(nc, *args, out)
    r = run_bass_kernel_spmd(nc, [arrays], core_ids=[0])
    return r.results[0]["out"].reshape(1, S, E)
```

```python
import concourse.bass as bass
from concourse import mybir
from contextlib import ExitStack

F32 = mybir.dt.float32
BF16 = mybir.dt.bfloat16
I32 = mybir.dt.int32
ACT = mybir.ActivationFunctionType
ALU = mybir.AluOpType
X_AXIS = mybir.AxisListType.X

P = 128
S = 4096
E = 256
H = 16
D = E // H
KH = E // P
TILES = S // P
EPS = 1e-5
PARTS = 3
SPLIT_ROWS = 6 * D
SHIFT_ROWS = SPLIT_ROWS + PARTS
QB = 512
NQB = S // QB
UNITS = H * NQB
QT = QB // P
KT = S // P
KCHUNK = 1024
NKC = S // KCHUNK
CHUNKS = QT * NKC
ITEMS = CHUNKS + 1
BATCH = 4
NBATCH = KT // BATCH
PV_LAG = 4
LATE = 1 + PV_LAG // BATCH
PBUFS = 16
STBUFS = 3
VCOL = 32
KBUFS = 3
DMA = 16

QUERY_GROUPS = ((0, 3, 0), (3, 2, 1), (5, 1, 2))
KEY_GROUPS = ((0, 3, 0), (3, 2, 0), (5, 1, 0))
N_EXPERTS = 8
F = 1024
FT = F // P
RB = 256
RT = RB // P
GBUFS = 4
BLOCKS = S // RB + N_EXPERTS - 1
SLOTS = BLOCKS * RB
COUNT_STEPS = S // RB


def wait(engine, sem, value):
    if not isinstance(value, int) or value > 0:
        engine.wait_ge(sem, value)


def wait_alone(engine, sem, value, turns):
    wait(engine, sem, value)
    engine.sem_inc(turns, 1)


def ring_base(step):
    return 0 if isinstance(step, int) and step == -2 else 33 + ITEMS * step


def build(nc, x, w_qk, w_vr, b_qk, b_vr, w_out, b_out, w1, b1, w2, b2,
          c_ident, c_identb, c_before, c_ones, c_route, c_tokens, out):
    ctx = ExitStack()
    with ctx:
        def sb(name, shape, dtype=F32):
            return ctx.enter_context(nc.sbuf_tensor(name, shape, dtype))

        def sem(name):
            return ctx.enter_context(nc.semaphore(name))

        q_parts = nc.dram_tensor("q_parts", (H, PARTS, D, S), BF16).ap()
        k_parts = nc.dram_tensor("k_parts", (H, PARTS, D, S), BF16).ap()

        token_rows = nc.dram_tensor("token_rows", (S + 1, 2, E), F32).ap()
        slot_tokens = nc.dram_tensor("slot_tokens", (SLOTS, 1), I32).ap()

        x_sb = sb("x_sb", [P, TILES, E])
        wide = sb("wide", [P, TILES, E])
        big = sb("big", [P, KH * S])
        xn, attn_out = wide, wide
        xnT = big[:, :].rearrange("p (k s) -> p k s", k=KH)
        probs = big[:, :].rearrange("p (b q) -> p b q", q=QB)
        v_all = sb("v_all", [P, H, KT, D])
        v_flat = v_all[:, :, :, :].rearrange("p h k d -> p (h k d)")
        w1_sb = v_flat[:, 0:2 * KH * F].rearrange("p (b k f) -> p b k f", b=2, k=KH)
        w2_sb = v_flat[:, 2 * KH * F:2 * KH * F + 2 * FT * E].rearrange("p (b f e) -> p b f e", b=2, f=FT)
        hT = big[:, 0:2 * FT * RB].rearrange("p (b f r) -> p b f r", b=2, f=FT)
        at = 2 * FT * RB
        xgT = big[:, at:at + 2 * KH * RB].rearrange("p (b k r) -> p b k r", b=2, k=KH)
        at += 2 * KH * RB
        y_sb = big[:, at:at + 2 * RT * E].rearrange("p (b r e) -> p b r e", b=2, r=RT)
        rows_g = wide[:, 0:GBUFS * RT * 2, :].rearrange("p (b r a) e -> p b r a e", b=GBUFS, r=RT)
        b1_all = sb("b1_all", [P, N_EXPERTS * FT])
        b1_sb = sb("b1_sb", [P, 2, FT])
        b2_sb = sb("b2_sb", [P, 2, E])
        before = sb("before", [P, P])
        ones = sb("ones", [P, P])
        route_c = sb("route_c", [P, N_EXPERTS * COUNT_STEPS + N_EXPERTS + BLOCKS])
        count_step = route_c[:, 0:N_EXPERTS * COUNT_STEPS].rearrange("p (e c) -> p e c", e=N_EXPERTS)
        first_wins = route_c[:, N_EXPERTS * COUNT_STEPS:N_EXPERTS * COUNT_STEPS + N_EXPERTS]
        block_no = route_c[:, N_EXPERTS * COUNT_STEPS + N_EXPERTS:]
        tokens = sb("tokens", [P, KT], I32)
        top = sb("top", [P, KT])
        one_hot = sb("one_hot", [P, KT, N_EXPERTS])
        ranks = sb("ranks", [P, 2, KT, N_EXPERTS])
        scan = sb("scan", [P, 2, KT, N_EXPERTS])
        over = sb("over", [P, N_EXPERTS, COUNT_STEPS])
        blocks = sb("blocks", [P, N_EXPERTS])
        block_end = sb("block_end", [P, 2, N_EXPERTS])
        block_cmp = sb("block_cmp", [P, BLOCKS, N_EXPERTS])
        block_sum = sb("block_sum", [P, BLOCKS])
        block_expert = sb("block_expert", [P, BLOCKS], I32)
        slots = sb("slots", [P, KT], I32)
        slot_now = sb("slot_now", [P, 1], I32)
        token_now = sb("token_now", [P, 1], I32)
        zero_row = sb("zero_row", [1, E])
        no_tokens = sb("no_tokens", [P, SLOTS // P], I32)
        slot_tok = sb("slot_tok", [P, SLOTS // P], I32)
        block_tokens = sb("block_tokens", [P, GBUFS, RT], I32)
        keys = sb("keys", [P, KBUFS * S], BF16)
        q_max = sb("q_max", [P, 2, QB], BF16)
        q_exp = sb("q_exp", [P, 2, QB], BF16)
        v_unit = sb("v_unit", [P, 2, KT, VCOL])
        chunk_max = sb("chunk_max", [P, QT, NKC])
        neg_max = sb("neg_max", [P, 2, QT])
        rest = sb("rest", [P, 2, QT])
        max_parts = sb("max_parts", [P, PARTS * QT], BF16)
        max_rows = sb("max_rows", [PARTS * QT, 2, P], BF16)
        o_pairs = sb("o_pairs", [P, QT, 2, D + 1])
        o_sum = sb("o_sum", [P, QT, D + 1])
        inv_sum = sb("inv_sum", [P, QT])
        wqk_sb = sb("wqk_sb", [P, KH, 2 * E])
        wvr_sb = sb("wvr_sb", [P, KH, E + N_EXPERTS])
        wout_sb = sb("wout_sb", [P, KH, E])
        bqk_sb = sb("bqk_sb", [P, 4])
        bvr_sb = sb("bvr_sb", [P, E + N_EXPERTS])
        bout_sb = sb("bout_sb", [P, E])
        ident = sb("ident", [P, P])
        identb = sb("identb", [P, P], BF16)
        stats = sb("stats", [P, TILES, 6])
        mean_var = sb("mean_var", [P, TILES, 2])
        var_eps = sb("var_eps", [P, TILES])
        std = sb("std", [P, TILES])
        rstd = sb("rstd", [P, TILES])
        newton = sb("newton", [P, TILES])
        newton2 = sb("newton2", [P, TILES])
        w_flat = wide[:, :, :].rearrange("p t e -> p (t e)")
        qk_f32 = w_flat[:, 0:4 * 512].rearrange("p (m s) -> p m s", m=4)
        qk_rest = w_flat[:, 4 * 512:8 * 512].rearrange("p (m s) -> p m s", m=4)
        qk_stage = w_flat[:, 8 * 512:14 * 512].bitcast(BF16).rearrange("p (m a s) -> p m a s", m=4, a=PARTS)
        pv_sb = sb("pv_sb", [P, QB])
        o_cols = sb("o_cols", [P, QB])
        scores = sb("scores", [P, KT, N_EXPERTS])
        oT = sb("oT", [P, 2, KH, P])

        ring = ctx.enter_context(nc.psum_tensor("ring", [P, 2, 2, 512], F32))
        st = ctx.enter_context(nc.psum_tensor("st", [P, STBUFS, 512], F32))
        pv = ctx.enter_context(nc.psum_tensor("pv", [P, 512], F32))

        def bank(n):
            return ring[:, n // 2, n % 2, :]

        x_loaded = [sem(f"x_loaded{c}") for c in range(4)]
        w_loaded = sem("w_loaded")
        vec = sem("vec")
        var_ready = sem("var_ready")
        std_ready = sem("std_ready")
        xn_ready = sem("xn_ready")
        tr_ready = sem("tr_ready")
        tr_copied = sem("tr_copied")
        v_ready = sem("v_ready")
        v_copied = sem("v_copied")
        qk_ready = sem("qk_ready")
        qk_f32_ready = sem("qk_f32_ready")
        qk_copied = sem("qk_copied")
        rest_ready = sem("rest_ready")
        part2_ready = sem("part2_ready")
        part3_ready = sem("part3_ready")
        stored = [sem(f"stored{n}") for n in range(4)]
        sp_turns = sem("sp_turns")
        pool_turns = sem("pool_turns")
        k_first = sem("k_first")
        k_loaded = sem("k_loaded")
        qm_loaded = [sem(f"qm_loaded{n}") for n in range(2)]
        qe_loaded = [sem(f"qe_loaded{n}") for n in range(2)]
        ones_ready = sem("ones_ready")
        ring_full = sem("ring_full")
        ring_free = sem("ring_free")
        st_ready = sem("st_ready")
        exp_done = sem("exp_done")
        pv_done = sem("pv_done")
        pv_copied = sem("pv_copied")
        neg_ready = sem("neg_ready")
        pool_own = sem("pool_own")
        parts_ready = sem("parts_ready")
        inv_ready = sem("inv_ready")
        o_ready = sem("o_ready")
        aux_copied = sem("aux_copied")
        pairs_summed = sem("pairs_summed")
        out_scaled = sem("out_scaled")
        v_unit_ready = sem("v_unit_ready")
        bias_added = sem("bias_added")
        ot_ready = sem("ot_ready")
        ot_copied = sem("ot_copied")
        proj_ready = sem("proj_ready")
        proj_added = sem("proj_added")
        xn_stored = sem("xn_stored")
        one_hot_ready = sem("one_hot_ready")
        ranks_ready = sem("ranks_ready")
        ranks_copied = sem("ranks_copied")
        slots_ready = sem("slots_ready")
        zeroed = sem("zeroed")
        zeros_stored = sem("zeros_stored")
        now_ready = sem("now_ready")
        scattered = sem("scattered")
        slot_tok_loaded = sem("slot_tok_loaded")
        w_ready = [sem(f"w_ready{n}") for n in range(2)]
        gather_ready = sem("gather_ready")
        gathered = [sem(f"gathered{n}") for n in range(2)]
        xgT_ready = sem("xgT_ready")
        xgT_copied = sem("xgT_copied")
        h_ready = sem("h_ready")
        gelu_done = sem("gelu_done")
        y_ready = sem("y_ready")
        y_copied = sem("y_copied")
        y_stored = [sem(f"y_stored{n}") for n in range(2)]
        y_biased = sem("y_biased")
        sum_stored = sem("sum_stored")

        xv = x.rearrange("(t p) e -> p t e", p=P)
        CH = TILES // 4
        SUM_STORES = ((0, CH), (CH, 2 * CH), (2 * CH, 3 * CH), (3 * CH, TILES - 2), (TILES - 2, TILES))
        W_LOADS = 13
        W_BLOCK = 4 * DMA
        QK_LOADS = 3 * DMA
        QE_LOADS = 2 * QK_LOADS

        block = ctx.enter_context(nc.Block())

        @block.sync
        def _(sp):
            for c in range(4):
                sp.dma_start(x_sb[:, c * CH:(c + 1) * CH, :], xv[:, c * CH:(c + 1) * CH, :]).then_inc(x_loaded[c], 16)
            sp.dma_start(ident[:, :], c_ident).then_inc(w_loaded, 16)
            sp.dma_start(identb[:, :], c_identb).then_inc(w_loaded, 16)
            sp.dma_start(wvr_sb[:, :, :], w_vr.rearrange("(k p) n -> p k n", p=P)).then_inc(w_loaded, 16)
            sp.dma_start(bvr_sb[:, :], b_vr.partition_broadcast(P)).then_inc(w_loaded, 16)
            sp.dma_start(wqk_sb[:, :, :], w_qk.rearrange("(k p) n -> p k n", p=P)).then_inc(w_loaded, 16)
            sp.dma_start(bqk_sb[:, :], b_qk).then_inc(w_loaded, 16)
            sp.dma_start(wout_sb[:, :, :], w_out.rearrange("(k p) n -> p k n", p=P)).then_inc(w_loaded, 16)
            sp.dma_start(bout_sb[:, :], b_out.partition_broadcast(P)).then_inc(w_loaded, 16)
            sp.dma_start(before[:, :], c_before).then_inc(w_loaded, 16)
            sp.dma_start(ones[:, :], c_ones).then_inc(w_loaded, 16)
            sp.dma_start(route_c[:, :], c_route.partition_broadcast(P)).then_inc(w_loaded, 16)
            sp.dma_start(tokens[:, :], c_tokens).then_inc(w_loaded, 16)
            sp.dma_start(b1_all[:, :], b1).then_inc(w_loaded, 16)
            for c in range(4):
                sp.wait_ge(xn_ready, (c + 1) * CH)
                sp.dma_start(token_rows[0:S, 0, :].rearrange("(t p) e -> p t e", p=P)[:, c * CH:(c + 1) * CH, :],
                             xn[:, c * CH:(c + 1) * CH, :]).then_inc(xn_stored, 16)
            sp.wait_ge(zeroed, 2)
            for half in range(2):
                sp.dma_start(token_rows[S:S + 1, half, :], zero_row[:, :]).then_inc(zeros_stored, 16)
            sp.dma_start(slot_tokens.rearrange("(p c) o -> p (c o)", p=P), no_tokens[:, :]).then_inc(zeros_stored, 16)

            def store_parts(nc_, mt):
                dst = (q_parts, q_parts, k_parts, k_parts)[mt]
                h0 = 8 * (mt % 2)
                wait_alone(sp, part3_ready, 4 * nc_ + mt + 1, sp_turns)
                for part in range(PARTS):
                    sp.dma_start(dst[h0:h0 + 8, part, :, bass.ds(nc_ * 512, 512)],
                                 qk_stage[:, mt, part, :]).then_inc(stored[mt], 16)

            with sp.Fori(0, S // 512) as nc_:
                for mt in range(4):
                    store_parts(nc_, mt)
            for n in range(4):
                wait(sp, stored[n], S // 512 * PARTS * DMA)

            def load_keys(head, at, signal):
                for g, n, part in KEY_GROUPS:
                    sp.dma_start(keys[g * D:(g + n) * D, at:at + S],
                                 k_parts[head, part:part + n, :, :].rearrange("a d s -> (a d) s")).then_inc(signal, 16)

            def load_queries(unit, to, signal):
                src = q_parts[bass.ds((unit >> 3) & 15, 1), :, :, bass.ds((unit & 7) * QB, QB)]
                for g, n, part in QUERY_GROUPS:
                    one = src[:, part:part + 1, :, :].rearrange("h a d s -> (h a) d s")
                    sp.dma_start(to[g * D:(g + n) * D, :], one.to_broadcast([n, D, QB])).then_inc(signal, 16)

            load_keys(0, 0, k_first)
            load_queries(0, q_max[:, 0, :], qm_loaded[0])
            load_queries(1, q_max[:, 1, :], qm_loaded[1])
            load_keys(1, S, k_loaded)

            def step(i, t, keys_too=True, exp=True, ahead=True):
                s = 2 * i + t
                if keys_too:
                    wait_alone(sp, k_loaded, QK_LOADS + QK_LOADS * s, sp_turns)
                    wait_alone(sp, st_ready, KT * s, sp_turns)
                    eighth = (s & 7) * 512
                    slot = ((s >> 3) + 2) % KBUFS
                    for g, n, part in KEY_GROUPS:
                        sp.dma_start(keys[g * D:(g + n) * D, bass.ds(slot * S + eighth, 512)],
                                     k_parts[bass.ds(((s >> 3) + 2) & 15, 1), part:part + n, :, bass.ds(eighth, 512)]
                                     .rearrange("h a d s -> (h a d) s")).then_inc(k_loaded, 16)
                if exp:
                    wait_alone(sp, st_ready, KT * s, sp_turns)
                    load_queries(s + 1, q_exp[:, 1 - t, :], qe_loaded[1 - t])
                if ahead:
                    wait_alone(sp, ring_full, ring_base(s), sp_turns)
                    load_queries((s + 3) & 127, q_max[:, 1 - t, :], qm_loaded[1 - t])
                if exp:
                    wait(sp, aux_copied, s + 2)
                    for part in range(PARTS):
                        sp.dma_start(q_exp[SPLIT_ROWS + part:SPLIT_ROWS + part + 1, 1 - t, :]
                                     .rearrange("a (q c) -> a q c", q=QT),
                                     max_rows[part * QT:(part + 1) * QT, 1 - t, :]).then_inc(qe_loaded[1 - t], 16)

            wait(sp, ring_full, 16)
            load_queries(2, q_max[:, 0, :], qm_loaded[0])
            step(-1, 1, keys_too=False, ahead=False)
            step(0, 0)
            step(0, 1)
            with sp.Fori(1, TILES + 2) as i:
                step(i, 0)
                step(i, 1)
            sp.wait_ge(scattered, TILES * 16)
            sp.dma_start(slot_tok[:, :], slot_tokens.rearrange("(c p) o -> p (c o)", p=P),
                         allow_slow_non_contiguous=True).then_inc(slot_tok_loaded, 16)
            with sp.Fori(TILES + 2, 63) as i:
                step(i, 0)
                step(i, 1)
            step(63, 0, keys_too=False, ahead=False)
            wait(sp, k_loaded, QK_LOADS + QK_LOADS * 126)
            wait(sp, qm_loaded[0], QK_LOADS * 65)

            def load_expert(b, t):
                e = sp.value_load(block_expert[0:1, bass.ds(b, 1)], min_val=0, max_val=N_EXPERTS - 1)
                sp.dma_start(w1_sb[:, t, :, :], w1[bass.ds(e, 1), :, :, :].rearrange("x p k f -> (x p) k f")).then_inc(w_ready[t], 16)
                sp.dma_start(w2_sb[:, t, :, :], w2[bass.ds(e, 1), :, :, :].rearrange("x p f e -> (x p) f e")).then_inc(w_ready[t], 16)
                sp.dma_start(b1_sb[:, t, :], b1_all[:, bass.ds(e * FT, FT)]).then_inc(w_ready[t], 16)
                sp.dma_start(b2_sb[:, t, :], b2[bass.ds(e, 1), :].rearrange("x e -> (x e)").partition_broadcast(P)).then_inc(w_ready[t], 16)

            sp.wait_ge(v_unit_ready, UNITS)
            load_expert(0, 0)
            load_expert(1, 1)
            for lo, hi in SUM_STORES:
                wait(sp, proj_added, hi)
                sp.dma_start(token_rows[0:S, 1, :].rearrange("(t p) e -> p t e", p=P)[:, lo:hi, :],
                             x_sb[:, lo:hi, :]).then_inc(sum_stored, 16)

            def expert_step(b, t):
                wait_alone(sp, y_copied, b + 1, sp_turns)
                load_expert(b + 2, t)

            with sp.Fori(0, (BLOCKS - 3) // 2) as i:
                expert_step(2 * i, 0)
                expert_step(2 * i + 1, 1)
            expert_step(BLOCKS - 3, 0)

        @block.tensor
        def _(pe):
            pe.wait_ge(w_loaded, W_LOADS * 16)

            def value_tile(kt):
                wait(pe, tr_copied, kt // 2 + 1)
                wait(pe, v_copied, kt - 2)
                for k in range(KH):
                    last = nc.tensor.matmul(st[:, kt % STBUFS, 0:E + N_EXPERTS], xnT[:, k, kt * P:(kt + 1) * P],
                                            wvr_sb[:, k, :], start=(k == 0), stop=(k == KH - 1))
                last.then_inc(v_ready, 1)

            for n in range(TILES // 2):
                pe.wait_ge(xn_ready, 2 * n + 2)
                wait(pe, tr_copied, n - 3)
                for k in range(KH):
                    for u in range(2):
                        last = nc.tensor.transpose(bank(n % 4)[:, (2 * k + u) * P:(2 * k + u + 1) * P],
                                                   xn[:, 2 * n + u, k * P:(k + 1) * P], ident[:, :])
                last.then_inc(tr_ready, 1)

            def qk_item(c, mt):
                wait(pe, qk_copied, 4 * c + mt - 3)
                for k in range(KH):
                    last = nc.tensor.matmul(bank(mt), wqk_sb[:, k, mt * P:(mt + 1) * P],
                                            xnT[:, k, bass.ds(c * 512, 512)], start=(k == 0), stop=(k == KH - 1))
                last.then_inc(qk_ready, 1)

            for mt in range(4):
                pe.wait_ge(tr_copied, TILES // 2 - 3 + mt)
                qk_item(0, mt)
            with pe.Fori(1, S // 512) as c:
                for mt in range(4):
                    qk_item(c, mt)
            for kt in range(TILES):
                value_tile(kt)
            pe.wait_ge(qk_copied, 32)
            pe.wait_ge(ones_ready, 3)

            def max_chunk(s, t, c, par, key0):
                if c == CHUNKS // 2 + 1:
                    wait(pe, aux_copied, s + 2)
                else:
                    wait(pe, ring_free, CHUNKS * (s + 2) + c - (1 if c != CHUNKS // 2 else 0))
                qt, kc = c // NKC, c % NKC
                for half in range(2):
                    last = nc.tensor.matmul(ring[:, par, half, :], q_max[0:SPLIT_ROWS, t, qt * P:(qt + 1) * P],
                                            keys[0:SPLIT_ROWS, bass.ds(key0 + kc * KCHUNK + half * 512, 512)],
                                            start=True, stop=True)
                last.then_inc(ring_full, 1)

            def aux(s, par, maxima, sums):
                wait(pe, ring_free, CHUNKS * (s + 2) + CHUNKS // 2 - 1 if not (isinstance(s, int) and s > 125) else CHUNKS * UNITS)
                wait(pe, aux_copied, s if isinstance(s, int) and s == UNITS else 0)
                if sums:
                    wait(pe, pv_copied, s)
                    for qt in range(QT):
                        last = nc.tensor.transpose(ring[:, par, 0, qt * P:(qt + 1) * P],
                                                   pv_sb[:, qt * P:(qt + 1) * P], ident[:, :])
                if maxima:
                    wait(pe, parts_ready, s + 2)
                    last = nc.tensor.transpose(ring[:, par, 1, :].bitcast(BF16)[0:PARTS * QT, 0:P],
                                               max_parts[:, :], identb[:, :])
                last.then_inc(ring_full, 1)

            def pv_batch(s, t, b):
                wait(pe, exp_done, KT * s + BATCH * (b + 1))
                if b == 0:
                    wait(pe, ranks_copied, 1)
                    wait(pe, pv_copied, s)
                    wait(pe, v_unit_ready, s + 1)
                for j in range(BATCH * b, BATCH * (b + 1)):
                    c = 32 * (j % 4)
                    last = nc.tensor.matmul(pv[c:c + VCOL, :], v_unit[:, t, j, :], probs[:, j % PBUFS, :],
                                            start=(j < 4), stop=(j >= KT - 4))
                last.then_inc(pv_done, 1)

            def step(i, t, maxima=True, exp=True, prev=True, aux_max=True, aux_sum=True, base=None):
                s = 2 * i + t
                base = ring_base(s) if base is None else base
                has_aux = aux_max or aux_sum
                if maxima:
                    wait(pe, qm_loaded[t], QK_LOADS * (i + 2))
                    wait(pe, k_first, QK_LOADS)
                    wait(pe, k_loaded, QK_LOADS if isinstance(s, int) and s < 2 else QK_LOADS * s)
                    max_keys = (((s + 2) >> 3) % KBUFS) * S
                if exp:
                    exp_keys = ((s >> 3) % KBUFS) * S
                    wait(pe, qe_loaded[t], QE_LOADS * (i + 1))
                k = 0
                first = (base % 2) if isinstance(base, int) else (1 + t) % 2
                for j in range(KT):
                    if exp:
                        if j == 0:
                            wait(pe, exp_done, KT * s - 1)
                        elif j == 1:
                            wait(pe, exp_done, KT * s)
                        elif j > 2:
                            wait(pe, exp_done, KT * s + j - 2)
                        nc.tensor.matmul(st[:, j % STBUFS, :], keys[0:SHIFT_ROWS, bass.ds(exp_keys + j * P, P)],
                                         q_exp[0:SHIFT_ROWS, t, :], start=True, stop=True).then_inc(st_ready, 1)
                    if maxima and j % 2 == 1:
                        max_chunk(s, t, j // 2, (first + k) % 2, max_keys)
                        k += 1
                    if j % BATCH == PV_LAG % BATCH:
                        b = (j - PV_LAG) // BATCH - 1
                        if b >= 0 and exp:
                            pv_batch(s, t, b)
                        if b < 0 and prev:
                            pv_batch(s - 1, 1 - t, NBATCH + b)
                    if j == CHUNKS and has_aux:
                        aux(s, (first + k) % 2, aux_max, aux_sum)
                        k += 1

            step(-1, 0, exp=False, prev=False, aux_max=False, aux_sum=False)
            pe.wait_ge(one_hot_ready, 1)
            oh = one_hot[:, :, :].rearrange("p t e -> p (t e)")
            nc.tensor.matmul(pv[:, 0:KT * N_EXPERTS], before[:, :], oh, start=True, stop=True)
            nc.tensor.matmul(pv[:, KT * N_EXPERTS:], ones[:, :], oh, start=True, stop=True).then_inc(ranks_ready, 1)
            pe.wait_ge(v_copied, TILES)
            step(-1, 1, exp=False, prev=False, aux_sum=False)
            step(0, 0, prev=False, aux_sum=False)
            step(0, 1)
            with pe.Fori(1, 63) as i:
                step(i, 0)
                step(i, 1)
            END = ring_base(126)
            step(63, 0, maxima=False)
            step(63, 1, maxima=False, aux_max=False, base=END + 1)
            for b in range(NBATCH - LATE, NBATCH):
                pv_batch(127, 1, b)
            aux(128, END % 2, False, True)

            def project(n):
                wait(pe, ot_copied, n + 1)
                wait(pe, proj_added, n - 1)
                for k in range(KH):
                    last = nc.tensor.matmul(bank(2 + n % 2)[:, 0:E], oT[:, n % 2, k, :], wout_sb[:, k, :],
                                            start=(k == 0), stop=(k == KH - 1))
                last.then_inc(proj_ready, 1)

            for n in range(TILES):
                wait(pe, ot_copied, n - 1)
                if n == 0:
                    pe.wait_ge(out_scaled, UNITS)
                for k in range(KH):
                    last = nc.tensor.transpose(bank(n % 2)[:, k * P:(k + 1) * P], attn_out[:, n, k * P:(k + 1) * P], ident[:, :])
                last.then_inc(ot_ready, 1)
                if n:
                    project(n - 1)
            project(TILES - 1)

            def turn_block(i, u):
                b = GBUFS * i + u
                wait(pe, gathered[u % 2], RT * DMA * (GBUFS // 2 * i + u // 2 + 1))
                wait(pe, xgT_copied, b)
                for k in range(KH):
                    for r in range(RT):
                        last = nc.tensor.transpose(st[:, 0, (k * RT + r) * P:(k * RT + r + 1) * P],
                                                   rows_g[:, u % GBUFS, r, 0, k * P:(k + 1) * P], ident[:, :])
                last.then_inc(xgT_ready, 1)

            def hidden(b, t, i):
                wait(pe, xgT_copied, b + 1)
                wait(pe, w_ready[t], W_BLOCK * (i + 1))
                for f in range(FT):
                    if f % 2 == 0:
                        wait(pe, gelu_done, (FT // 2) * (b - 1) + f // 2 + 1)
                    for k in range(KH):
                        last = nc.tensor.matmul(bank(f // 2)[:, (f % 2) * RB:(f % 2 + 1) * RB], w1_sb[:, t, k, f * P:(f + 1) * P],
                                                xgT[:, t, k, :], start=(k == 0), stop=(k == KH - 1))
                    if f % 2:
                        last.then_inc(h_ready, 1)

            def output(b, t):
                wait(pe, y_copied, b - 1)
                for r in range(RT):
                    for f in range(FT):
                        if r == 0 and f % 2 == 0:
                            wait(pe, gelu_done, (FT // 2) * b + f // 2 + 1)
                        last = nc.tensor.matmul(st[:, 1 + t, r * E:(r + 1) * E], hT[:, t, f, r * P:(r + 1) * P],
                                                w2_sb[:, t, f, :], start=(f == 0), stop=(f == FT - 1))
                last.then_inc(y_ready, 1)

            def expert_step(i, u, ahead=True):
                b, t = GBUFS * i + u, u % 2
                hidden(b, t, GBUFS // 2 * i + u // 2)
                if ahead:
                    turn_block(i, u + 1)
                output(b, t)

            pe.wait_ge(proj_added, TILES)
            turn_block(0, 0)
            for u in range(GBUFS):
                expert_step(0, u)
            with pe.Fori(1, BLOCKS // GBUFS) as i:
                for u in range(GBUFS):
                    expert_step(i, u)
            for u in range(BLOCKS % GBUFS):
                expert_step(BLOCKS // GBUFS, u, ahead=(u < BLOCKS % GBUFS - 1))

        @block.scalar
        def _(act):
            for c in range(4):
                act.wait_ge(var_ready, c + 1)
                nc.scalar.activation(std[:, c * CH:(c + 1) * CH], var_eps[:, c * CH:(c + 1) * CH], ACT.Sqrt).then_inc(std_ready, 1)
            for n in range(TILES // 2):
                act.wait_ge(tr_ready, n + 1)
                nc.scalar.activation(xnT[:, :, n * 2 * P:(n + 1) * 2 * P],
                                     bank(n % 4).rearrange("p (k s) -> p k s", k=KH), ACT.Copy).then_inc(tr_copied, 1)

            def qk_item(c, mt):
                n = 4 * c + mt
                wait(act, qk_ready, n + 1)
                wait(act, rest_ready, n - 3)
                nc.scalar.activation(qk_f32[:, mt, :], bank(mt), ACT.Identity, bias=bqk_sb[:, mt:mt + 1]).then_inc(qk_f32_ready, 1)
                wait(act, stored[mt], DMA * PARTS * c)
                nc.scalar.activation(qk_stage[:, mt, 0, :], bank(mt), ACT.Identity, bias=bqk_sb[:, mt:mt + 1]).then_inc(qk_copied, 1)

            act.wait_ge(w_loaded, W_LOADS * 16)
            act.wait_ge(xn_stored, 4 * 16)
            for mt in range(4):
                qk_item(0, mt)
            with act.Fori(1, S // 512) as c:
                for mt in range(4):
                    qk_item(c, mt)

            def copy_pv(s):
                wait(act, pv_done, NBATCH * s)
                if not (isinstance(s, int) and s < 2):
                    wait(act, ring_full, ring_base(s) - 8 if not (isinstance(s, int) and s > 126) else ring_base(126) + s - 126)
                nc.scalar.activation(pv_sb[:, :], pv[:, :], ACT.Copy).then_inc(pv_copied, 1)

            def aux(s, t, n, maxima, sums):
                wait(act, ring_full, n + 1)
                if maxima:
                    wait(act, qe_loaded[1 - t], QE_LOADS * ((s + 1) >> 1))
                    last = nc.scalar.activation(max_rows[:, 1 - t, :], aux_bank(n)[1].bitcast(BF16)[0:PARTS * QT, 0:P], ACT.Copy)
                if sums:
                    wait(act, pairs_summed, s - 1)
                    last = nc.scalar.activation(o_cols[:, :], aux_bank(n)[0], ACT.Copy)
                last.then_inc(aux_copied, 1)

            def aux_bank(n):
                par = n % 2 if isinstance(n, int) else aux_par[0]
                return ring[:, par, 0, :], ring[:, par, 1, :]

            aux_par = [0]

            def step(i, t, prev=True, aux_max=True, aux_sum=True, aux_n=None):
                s = 2 * i + t
                for j in range(KT):
                    if j == CHUNKS + 1:
                        aux_par[0] = (1 + t + CHUNKS // 2) % 2
                        aux(s, t, ring_base(s) + CHUNKS // 2 if aux_n is None else aux_n, aux_max, aux_sum)
                    wait(act, st_ready, KT * s + j + 1)
                    wait(act, pv_done, NBATCH * s + j // BATCH + 1 - PBUFS // BATCH)
                    nc.scalar.activation(probs[:, j % PBUFS, :], st[:, j % STBUFS, :], ACT.Exp, scale=0.25).then_inc(exp_done, 1)
                    if j == PV_LAG + 1 and prev:
                        copy_pv(s)

            END = ring_base(126)
            aux(-1, 1, ring_base(-1) + CHUNKS // 2, True, False)
            step(0, 0, prev=False, aux_sum=False)
            step(0, 1)
            with act.Fori(1, 63) as i:
                step(i, 0)
                step(i, 1)
            step(63, 0, aux_n=END)
            step(63, 1, aux_max=False, aux_n=END + 1)
            copy_pv(128)
            aux(128, 0, END + 2, False, True)

            for n in range(TILES):
                act.wait_ge(ot_ready, n + 1)
                wait(act, proj_ready, n - 1)
                nc.scalar.activation(oT[:, n % 2, :, :].rearrange("p k s -> p (k s)"), bank(n % 2)[:, 0:KH * P], ACT.Copy).then_inc(ot_copied, 1)

            def expert_step(i, t):
                b = 2 * i + t
                wait(act, w_ready[t], W_BLOCK * (i + 1))
                wait(act, y_ready, b - 1)
                for f in range(FT):
                    if f % 2 == 0:
                        wait(act, h_ready, (FT // 2) * b + f // 2 + 1)
                    ins = nc.scalar.activation(hT[:, t, f, :], bank(f // 2)[:, (f % 2) * RB:(f % 2 + 1) * RB],
                                               ACT.Gelu, bias=b1_sb[:, t, f:f + 1])
                    if f % 2:
                        ins.then_inc(gelu_done, 1)

            expert_step(0, 0)
            expert_step(0, 1)
            with act.Fori(1, BLOCKS // 2) as i:
                expert_step(i, 0)
                expert_step(i, 1)
            expert_step(BLOCKS // 2, 0)

        @block.vector
        def _(dve):
            count = [0]

            def chained(ins):
                count[0] += 1
                ins.then_inc(vec, 1)
                dve.wait_ge(vec, count[0])

            def normalise(c):
                lo, hi = c * CH, (c + 1) * CH
                dve.wait_ge(std_ready, c + 1)
                chained(nc.vector.reciprocal(rstd[:, lo:hi], std[:, lo:hi]))
                chained(nc.vector.tensor_tensor(newton[:, lo:hi], rstd[:, lo:hi], rstd[:, lo:hi], ALU.mult))
                chained(nc.vector.tensor_tensor(newton2[:, lo:hi], newton[:, lo:hi], var_eps[:, lo:hi], ALU.mult))
                chained(nc.vector.tensor_scalar(newton[:, lo:hi], newton2[:, lo:hi], -0.5, 1.5, ALU.mult, ALU.add))
                chained(nc.vector.tensor_tensor(std[:, lo:hi], rstd[:, lo:hi], newton[:, lo:hi], ALU.mult))
                for n in range(lo, hi):
                    nc.vector.tensor_scalar(xn[:, n, :], x_sb[:, n, :], mean_var[:, n, 0:1], std[:, n:n + 1],
                                            ALU.subtract, ALU.mult).then_inc(xn_ready, 1)

            for c in range(4):
                lo, hi = c * CH, (c + 1) * CH
                dve.wait_ge(x_loaded[c], 16)
                for n in range(lo, hi):
                    ins = nc.vector.bn_stats(stats[:, n, :], x_sb[:, n, :])
                    ins.then_inc(vec, 1)
                    count[0] += 1
                dve.wait_ge(vec, count[0])
                for n in range(lo, hi):
                    ins = nc.vector.bn_aggr(mean_var[:, n, :], stats[:, n, :])
                    ins.then_inc(vec, 1)
                    count[0] += 1
                dve.wait_ge(vec, count[0])
                nc.vector.tensor_scalar(var_eps[:, lo:hi], mean_var[:, lo:hi, 1], EPS, None, ALU.add).then_inc(var_ready, 1)
                if c:
                    normalise(c - 1)
            normalise(3)

            def qk_item(c, mt):
                n = 4 * c + mt
                wait(dve, qk_f32_ready, n + 1)
                wait(dve, qk_copied, n + 1)
                wait(dve, part3_ready, n - 3)
                nc.vector.tensor_tensor(qk_rest[:, mt, :], qk_f32[:, mt, :], qk_stage[:, mt, 0, :], ALU.subtract).then_inc(rest_ready, 1)
                wait(dve, rest_ready, n + 1)
                nc.vector.tensor_copy(qk_stage[:, mt, 1, :], qk_rest[:, mt, :]).then_inc(part2_ready, 1)

            for mt in range(4):
                qk_item(0, mt)
            with dve.Fori(1, S // 512) as c:
                for mt in range(4):
                    qk_item(c, mt)

            dve.wait_ge(w_loaded, W_LOADS * 16)
            for kt in range(TILES):
                dve.wait_ge(v_ready, kt + 1)
                b = st[:, kt % STBUFS, :]
                nc.vector.tensor_tensor(v_all[:, :, kt, :], b[:, 0:E].rearrange("p (h d) -> p h d", h=H),
                                        bvr_sb[:, 0:E].rearrange("p (h d) -> p h d", h=H), ALU.add)
                nc.vector.tensor_tensor(scores[:, kt, :], b[:, E:E + N_EXPERTS], bvr_sb[:, E:E + N_EXPERTS], ALU.add).then_inc(v_copied, 1)

            def over_experts(a):
                return a.unsqueeze(2).to_broadcast([P, a.shape[1], N_EXPERTS])

            def over_rows(a, n):
                return a.unsqueeze(1).to_broadcast([P, n, N_EXPERTS])

            dve.wait_ge(v_copied, TILES)
            chained(nc.vector.tensor_reduce(top[:, :], scores[:, :, :], axis=X_AXIS, op=ALU.max))
            chained(nc.vector.tensor_tensor(scan[:, 0, :, :], scores[:, :, :], over_experts(top[:, :]), ALU.is_equal))
            chained(nc.vector.tensor_tensor(scan[:, 1, :, :], scan[:, 0, :, :], over_rows(first_wins, KT), ALU.mult))
            chained(nc.vector.tensor_reduce(top[:, :], scan[:, 1, :, :], axis=X_AXIS, op=ALU.max))
            nc.vector.tensor_tensor(one_hot[:, :, :], over_rows(first_wins, KT), over_experts(top[:, :]), ALU.is_equal).then_inc(one_hot_ready, 1)

            def max_chunk(c, n, par):
                wait(dve, ring_full, n + 1)
                nc.vector.tensor_reduce(chunk_max[:, c // NKC, c % NKC:c % NKC + 1], ring[:, par, :, :].rearrange("p a b -> p (a b)"),
                                        axis=X_AXIS, op=ALU.max).then_inc(ring_free, 1)

            def invert(s):
                wait(dve, o_ready, s)
                nc.vector.reciprocal(inv_sum[:, :], o_sum[:, :, D]).then_inc(inv_ready, 1)

            def step(i, t, aux_max=True, aux_sum=True, between={}):
                s = 2 * i + t
                base = ring_base(s)
                first = (base % 2) if isinstance(base, int) else (1 + t) % 2
                k = 0
                wait(dve, neg_ready, s + 2)
                for c in range(CHUNKS):
                    if c == CHUNKS // 2 and (aux_max or aux_sum):
                        k += 1
                    if c in between:
                        between[c]()
                    if c == CHUNKS - 2 and aux_sum:
                        invert(s)
                    max_chunk(c, base + k, (first + k) % 2)
                    k += 1
                wait(dve, ring_free, CHUNKS * (s + 3))
                nc.vector.tensor_reduce(neg_max[:, t, :], chunk_max[:, :, :], axis=X_AXIS, op=ALU.max, negate=True).then_inc(neg_ready, 1)

            def sum_tiles():
                rank, total = ranks[:, 0, :, :], ranks[:, 1, :, :]
                src = total
                for n, shift in enumerate((1, 2, 4, 8, 16)):
                    dst = scan[:, n % 2, :, :]
                    chained(nc.vector.tensor_copy(dst[:, 0:shift, :], src[:, 0:shift, :]))
                    chained(nc.vector.tensor_tensor(dst[:, shift:, :], src[:, shift:, :], src[:, 0:KT - shift, :], ALU.add))
                    src = dst

            def count_blocks():
                src = scan[:, 0, :, :]
                counts = src[:, KT - 1, :]
                chained(nc.vector.tensor_tensor(over[:, :, :], counts.unsqueeze(2).to_broadcast([P, N_EXPERTS, COUNT_STEPS]), count_step, ALU.is_gt))
                chained(nc.vector.tensor_reduce(blocks[:, :], over[:, :, :], axis=X_AXIS, op=ALU.add))
                bsrc = blocks[:, :]
                for n, shift in enumerate((1, 2, 4)):
                    bdst = block_end[:, n % 2, :]
                    chained(nc.vector.tensor_copy(bdst[:, 0:shift], bsrc[:, 0:shift]))
                    chained(nc.vector.tensor_tensor(bdst[:, shift:], bsrc[:, shift:], bsrc[:, 0:N_EXPERTS - shift], ALU.add))
                    bsrc = bdst
                chained(nc.vector.tensor_tensor(block_cmp[:, :, :], over_experts(block_no), over_rows(bsrc, BLOCKS), ALU.is_ge))
                chained(nc.vector.tensor_reduce(block_sum[:, :], block_cmp[:, :, :], axis=X_AXIS, op=ALU.add))
                chained(nc.vector.tensor_scalar(block_expert[:, :], block_sum[:, :], float(N_EXPERTS - 1), None, ALU.min))

            def place_tokens():
                rank, total = ranks[:, 0, :, :], ranks[:, 1, :, :]
                src, bsrc = scan[:, 0, :, :], block_end[:, 0, :]
                other = scan[:, 1, :, :]
                chained(nc.vector.tensor_tensor(blocks[:, :], bsrc, blocks[:, :], ALU.subtract))
                chained(nc.vector.tensor_scalar(blocks[:, :], blocks[:, :], float(RB), None, ALU.mult))
                chained(nc.vector.tensor_tensor(other, src, total, ALU.subtract))
                chained(nc.vector.tensor_tensor(other, other, rank, ALU.add))
                chained(nc.vector.tensor_tensor(other, other, over_rows(blocks[:, :], KT), ALU.add))
                chained(nc.vector.tensor_tensor(other, other, one_hot[:, :, :], ALU.mult))
                chained(nc.vector.tensor_reduce(top[:, :], other, axis=X_AXIS, op=ALU.add))
                nc.vector.tensor_copy(slots[:, :], top[:, :]).then_inc(slots_ready, 1)

            step(-1, 0, aux_max=False, aux_sum=False)
            dve.wait_ge(ranks_ready, 1)
            nc.vector.tensor_copy(ranks[:, :, :, :].rearrange("p a t e -> p (a t e)"), pv[:, :]).then_inc(ranks_copied, 1)
            step(-1, 1, aux_sum=False)
            dve.wait_ge(ranks_copied, 1)
            step(0, 0, aux_sum=False, between={6: sum_tiles})
            step(0, 1, between={3: count_blocks, 10: place_tokens})
            with dve.Fori(1, 63) as i:
                step(i, 0)
                step(i, 1)
            for s in (126, 127, 128):
                invert(s)

            dve.wait_ge(bias_added, TILES)
            for n in range(TILES):
                dve.wait_ge(proj_ready, n + 1)
                nc.vector.tensor_tensor(x_sb[:, n, :], bank(2 + n % 2)[:, 0:E], x_sb[:, n, :], ALU.add).then_inc(proj_added, 1)

            def turned(b, t):
                wait(dve, xgT_ready, b + 1)
                wait(dve, h_ready, (FT // 2) * (b - 1))
                nc.vector.tensor_copy(xgT[:, t, :, :].rearrange("p k r -> p (k r)"), st[:, 0, :]).then_inc(xgT_copied, 1)

            def expert_step(i, t, ahead=True):
                b = 2 * i + t
                if ahead:
                    turned(b + 1, 1 - t)
                wait(dve, y_stored[t], RT * DMA * i)
                wait(dve, w_ready[t], W_BLOCK * (i + 1))
                wait(dve, y_ready, b + 1)
                nc.vector.tensor_tensor(y_sb[:, t, :, :], st[:, 1 + t, :].rearrange("p (r e) -> p r e", r=RT),
                                        b2_sb[:, t, :].unsqueeze(1).to_broadcast([P, RT, E]), ALU.add).then_inc(y_biased, 1)
                wait(dve, gathered[t], RT * DMA * (i + 1))
                wait(dve, y_biased, b + 1)
                nc.vector.tensor_tensor(y_sb[:, t, :, :], y_sb[:, t, :, :],
                                        rows_g[:, bass.ds(b & (GBUFS - 1), 1), :, 1, :].rearrange("p b r e -> p (b r) e"),
                                        ALU.add).then_inc(y_copied, 1)

            turned(0, 0)
            expert_step(0, 0)
            expert_step(0, 1)
            with dve.Fori(1, BLOCKS // 2) as i:
                expert_step(i, 0)
                expert_step(i, 1)
            expert_step(BLOCKS // 2, 0, ahead=False)

        @block.gpsimd
        def _(pool):
            nc.gpsimd.memset(no_tokens[:, :], S).then_inc(zeroed, 1)
            pool.wait_ge(zeroed, 1)
            nc.gpsimd.memset(zero_row[:, :], 0.0).then_inc(zeroed, 1)
            pool.wait_ge(zeroed, 2)
            nc.gpsimd.memset(keys[SPLIT_ROWS:SHIFT_ROWS, :], 1.0).then_inc(ones_ready, 1)
            pool.wait_ge(ones_ready, 1)
            nc.gpsimd.memset(v_unit[:, :, :, D:D + 1], 1.0).then_inc(ones_ready, 1)
            pool.wait_ge(ones_ready, 2)
            nc.gpsimd.memset(v_unit[:, :, :, D + 1:VCOL], 0.0).then_inc(ones_ready, 1)

            def qk_item(c, mt):
                n = 4 * c + mt
                wait(pool, part2_ready, n + 1)
                nc.gpsimd.tensor_tensor(qk_stage[:, mt, 2, :], qk_rest[:, mt, :], qk_stage[:, mt, 1, :], ALU.subtract).then_inc(part3_ready, 1)

            with pool.Fori(0, S // 512) as c:
                for mt in range(4):
                    qk_item(c, mt)
            pool.wait_ge(xn_ready, TILES)
            pool.wait_ge(w_loaded, W_LOADS * 16)

            def values(u, to):
                wait_alone(pool, pv_done, NBATCH * (u - 1), pool_turns)
                nc.gpsimd.tensor_copy(v_unit[:, to, :, 0:D], v_all[:, bass.ds((u >> 3) & 15, 1), :, :].rearrange("p h k d -> p (h k) d")).then_inc(v_unit_ready, 1)

            def step(i, t, sums=True):
                u = 2 * i + t + 1
                wait_alone(pool, neg_ready, u + 1, pool_turns)
                nm = neg_max[:, 1 - t, :]
                p = [max_parts[:, n * QT:(n + 1) * QT] for n in range(PARTS)]
                nc.gpsimd.tensor_copy(p[0], nm).then_inc(pool_own, 1)
                wait(pool, pool_own, 3 * u + 1)
                nc.gpsimd.tensor_tensor(rest[:, 0, :], nm, p[0], ALU.subtract).then_inc(pool_own, 1)
                wait_alone(pool, pool_own, 3 * u + 2, pool_turns)
                nc.gpsimd.tensor_copy(p[1], rest[:, 0, :]).then_inc(pool_own, 1)
                wait(pool, pool_own, 3 * u + 3)
                nc.gpsimd.tensor_tensor(p[2], rest[:, 0, :], p[1], ALU.subtract).then_inc(parts_ready, 1)
                values(u, 1 - t)
                if sums:
                    scale(u - 1)

            def scale(s):
                o = o_cols[:, :].rearrange("p (q g v) -> p q g v", q=QT, g=P // VCOL)[:, :, :, 0:D + 1]
                wait(pool, aux_copied, s + 2)
                nc.gpsimd.tensor_tensor(o_pairs[:, :, :, :], o[:, :, 0:2, :], o[:, :, 2:4, :], ALU.add).then_inc(pairs_summed, 1)
                wait(pool, pairs_summed, s)
                nc.gpsimd.tensor_tensor(o_sum[:, :, :], o_pairs[:, :, 0, :], o_pairs[:, :, 1, :], ALU.add).then_inc(o_ready, 1)
                if isinstance(s, int) and s == 1:
                    pool.wait_ge(xn_stored, 4 * 16)
                wait_alone(pool, inv_ready, s, pool_turns)
                u = s - 1
                nc.gpsimd.tensor_tensor(attn_out[:, bass.ds((u & 7) * QT, QT), bass.ds(((u >> 3) & 15) * D, D)],
                                        o_sum[:, :, 0:D], inv_sum[:, :].unsqueeze(2).to_broadcast([P, QT, D]), ALU.mult).then_inc(out_scaled, 1)

            pool.wait_ge(v_copied, TILES)
            step(-1, 1, sums=False)
            step(0, 0, sums=False)
            step(0, 1)
            pool.wait_ge(slots_ready, 1)
            pool.wait_ge(zeros_stored, 3 * 16)
            with pool.Fori(1, TILES + 1) as i:
                step(i, 0)
                nc.gpsimd.tensor_copy(slot_now[:, :], slots[:, bass.ds(i - 1, 1)]).then_inc(now_ready, 1)
                nc.gpsimd.tensor_copy(token_now[:, :], tokens[:, bass.ds(i - 1, 1)]).then_inc(now_ready, 1)
                wait_alone(pool, now_ready, 2 * i, pool_turns)
                nc.gpsimd.indirect_dma_start(out=slot_tokens, out_offset=bass.IndirectOffsetOnAxis(ap=slot_now[:, :], axis=0),
                                             in_=token_now[:, :], in_offset=None).then_inc(scattered, 16)
                step(i, 1)
                wait_alone(pool, scattered, DMA * i, pool_turns)
                tile_n = x_sb[:, bass.ds(i - 1, 1), :].rearrange("p n e -> p (n e)")
                nc.gpsimd.tensor_tensor(tile_n, tile_n, bout_sb[:, :], ALU.add).then_inc(bias_added, 1)
            with pool.Fori(TILES + 1, 63) as i:
                step(i, 0)
                step(i, 1)
            step(63, 0)
            scale(127)
            scale(128)

            def gather(b, u, i):
                t = u % 2
                wait_alone(pool, xgT_ready, b - 1, pool_turns)
                wait_alone(pool, y_copied, b - GBUFS + 1, pool_turns)
                wait_alone(pool, y_stored[t], RT * DMA * (i - 1), pool_turns)
                nc.gpsimd.tensor_copy(block_tokens[:, u, :], slot_tok[:, bass.ds(b * RT, RT)]).then_inc(gather_ready, 1)
                wait_alone(pool, gather_ready, b + 1, pool_turns)
                for r in range(RT):
                    nc.gpsimd.indirect_dma_start(out=rows_g[:, u, r, :, :].rearrange("p a e -> p (a e)"), out_offset=None,
                                                 in_=token_rows.rearrange("s a e -> s (a e)"),
                                                 in_offset=bass.IndirectOffsetOnAxis(ap=block_tokens[:, u, r:r + 1], axis=0)).then_inc(gathered[t], 16)

            def scatter(b, u):
                t = u % 2
                wait_alone(pool, y_copied, b + 1, pool_turns)
                for r in range(RT):
                    nc.gpsimd.indirect_dma_start(out=out, out_offset=bass.IndirectOffsetOnAxis(ap=block_tokens[:, u, r:r + 1], axis=0),
                                                 in_=y_sb[:, t, r, :], in_offset=None, bounds_check=S - 1, oob_is_err=False).then_inc(y_stored[t], 16)

            def blocks_of(i, count):
                for u in range(count):
                    gather(GBUFS * i + u + 2, (u + 2) % GBUFS, i * (GBUFS // 2) + (u + 2) // 2)
                    scatter(GBUFS * i + u, u)

            pool.wait_ge(slot_tok_loaded, 16)
            pool.wait_ge(sum_stored, len(SUM_STORES) * 16)
            gather(0, 0, 0)
            gather(1, 1, 0)
            blocks_of(0, GBUFS)
            with pool.Fori(1, (BLOCKS - 2) // GBUFS) as i:
                blocks_of(i, GBUFS)
            blocks_of((BLOCKS - 2) // GBUFS, (BLOCKS - 2) % GBUFS)
            scatter(BLOCKS - 2, (BLOCKS - 2) % GBUFS)
            scatter(BLOCKS - 1, (BLOCKS - 1) % GBUFS)
            pool.wait_ge(y_stored[0], RT * DMA * (BLOCKS // 2 + 1))
            pool.wait_ge(y_stored[1], RT * DMA * (BLOCKS // 2))


def kernel(**inputs):
    import numpy as np
    import concourse.bacc as bacc
    from concourse.bass_utils import run_bass_kernel_spmd

    a = {n: np.asarray(v) for n, v in inputs.items()}
    wqkv = a["L0_attn_Wqkv"].reshape(E, H, 3, D)
    bqkv = a["L0_attn_bqkv"].reshape(H, 3, D)
    import ml_dtypes
    arrays = {
        "x": a["L0_attn_x"].reshape(S, E),
        "w_qk": np.concatenate([wqkv[:, :, n, :].reshape(E, E) for n in (0, 1)], axis=1),
        "w_vr": np.concatenate([wqkv[:, :, 2, :].reshape(E, E), a["L0_ffn_wr"]], axis=1),
        "b_qk": np.ascontiguousarray(np.concatenate([bqkv[:, n, :].reshape(E) for n in (0, 1)]).reshape(4, P).T),
        "b_vr": np.concatenate([bqkv[:, 2, :].reshape(E), a["L0_ffn_br"]]),
        "w_out": a["L0_attn_Wout"],
        "b_out": a["L0_attn_bout"],
        "w1": a["L0_ffn_w1"].reshape(N_EXPERTS, KH, P, F).transpose(0, 2, 1, 3),
        "b1": a["L0_ffn_b1"].reshape(N_EXPERTS * FT, P).T,
        "w2": a["L0_ffn_w2"].reshape(N_EXPERTS, FT, P, E).transpose(0, 2, 1, 3),
        "b2": a["L0_ffn_b2"],
        "c_ident": np.eye(P, dtype=np.float32),
        "c_identb": np.eye(P, dtype=ml_dtypes.bfloat16),
        "c_before": np.triu(np.ones((P, P), np.float32), 1),
        "c_ones": np.ones((P, P), np.float32),
        "c_route": np.concatenate([np.tile(RB * np.arange(COUNT_STEPS), N_EXPERTS), N_EXPERTS - np.arange(N_EXPERTS),
                                   np.arange(BLOCKS)]).astype(np.float32),
        "c_tokens": np.arange(S, dtype=np.int32).reshape(TILES, P).T,
    }
    arrays = {n: np.ascontiguousarray(v) for n, v in arrays.items()}
    nc = bacc.Bacc("TRN2", target_bir_lowering=False, num_devices=1)
    args = [nc.dram_tensor(n, v.shape, mybir.dt.from_np(v.dtype), kind="ExternalInput").ap() for n, v in arrays.items()]
    out = nc.dram_tensor("out", (S, E), F32, kind="ExternalOutput").ap()
    build(nc, *args, out)
    r = run_bass_kernel_spmd(nc, [arrays], core_ids=[0])
    return r.results[0]["out"].reshape(1, S, E)
```
